# Optimizing a Trainium2 kernel written in Bass

```python
import numpy as np
import jax
import jax.numpy as jnp

def _softmax(x, axis=-1):
    return jax.nn.softmax(x, axis=axis)
def _gelu(x):
    return jax.nn.gelu(x, approximate=True)
def _silu(x):
    return jax.nn.silu(x)
def _sigmoid(x):
    return jax.nn.sigmoid(x)
def _layernorm(x, axis=-1, eps=1e-5):
    m = jnp.mean(x, axis=axis, keepdims=True)
    v = jnp.var(x, axis=axis, keepdims=True)
    return (x - m) / jnp.sqrt(v + eps)
def _scatter_add(tgt, idx, src, axis=0):
    return tgt.at[idx].add(src)
def _segment_sum(src, seg, n):
    return jax.ops.segment_sum(src, seg, n)

kernel_name = 'mk_conv_seq_d2_conv_nchw256_842cee'

def setup_inputs(seed: int = 0):
    np.random.seed(seed)
    _w = jnp.asarray
    def _rec_inputs():
        import jax
        import jax.numpy as jnp
        _gk = jax.random.key(seed)
        x = -0.0002928 + 1 * jax.random.normal(jax.random.fold_in(_gk, 1), (4, 256, 64, 64), jnp.float32)
        return x
    x = _rec_inputs()
    def _L0_conv_setup():
        import jax, jax.numpy as jnp
        import numpy as np
        B, C, H, W = (4, 256, 64, 64)
        CQK = C // 8
        key = jax.random.key(seed)
        ks = jax.random.split(key, 5)
        x = jax.random.normal(ks[0], (B, C, H, W), dtype=jnp.float32)
        Wq = jax.random.normal(ks[1], (CQK, C), dtype=jnp.float32) * (1.0 / np.sqrt(C))
        Wk = jax.random.normal(ks[2], (CQK, C), dtype=jnp.float32) * (1.0 / np.sqrt(C))
        Wv = jax.random.normal(ks[3], (C, C), dtype=jnp.float32) * (1.0 / np.sqrt(C))
        Wo = jax.random.normal(ks[4], (C, C), dtype=jnp.float32) * (1.0 / np.sqrt(C))
        gamma = jnp.ones((1,), dtype=jnp.float32)
        return {'x': x, 'Wq': Wq, 'Wk': Wk, 'Wv': Wv, 'Wo': Wo, 'gamma': gamma}
    _L0_conv_all = _L0_conv_setup()
    _L0_conv_in = {k: v for k, v in _L0_conv_all.items() if k in ('Wq', 'Wk', 'Wv', 'Wo', 'gamma', )}
    del _L0_conv_all

    def _L1_conv_setup():
        import jax, jax.numpy as jnp
        import numpy as np
        EPS = 1e-05

        def _bn(x, gamma, beta, mean, var):
            scale = gamma * jax.lax.rsqrt(var + EPS)
            return (x - mean[:, None, None]) * scale[:, None, None] + beta[:, None, None]

        def _prelu(x, alpha):
            a = alpha[0]
            return jnp.where(x >= 0, x, a * x)

        def _up2_nearest(x):
            return jnp.repeat(jnp.repeat(x, 2, axis=2), 2, axis=3)
        key = jax.random.key(seed)
        ks = jax.random.split(key, 12)
        B, C, H, W = (8, 256, 192, 192)
        x = jax.random.normal(ks[0], (B, C, H, W), dtype=jnp.float32)
        mag_w = jax.random.normal(ks[1], (C, C), dtype=jnp.float32) * (1.0 / np.sqrt(C))
        mag_b = jax.random.normal(ks[2], (C,), dtype=jnp.float32) * 0.01
        phase_w = jax.random.normal(ks[3], (2 * C, 2 * C), dtype=jnp.float32) * (1.0 / np.sqrt(2 * C))
        phase_b = jax.random.normal(ks[4], (2 * C,), dtype=jnp.float32) * 0.01
        mag_gamma = jnp.ones((C,), jnp.float32)
        mag_beta = jnp.zeros((C,), jnp.float32)
        mag_mean = jax.random.normal(ks[5], (C,), dtype=jnp.float32) * 0.1
        mag_var = jax.random.uniform(ks[6], (C,), jnp.float32, 0.5, 1.5)
        phase_gamma = jnp.ones((2 * C,), jnp.float32)
        phase_beta = jnp.zeros((2 * C,), jnp.float32)
        phase_mean = jax.random.normal(ks[7], (2 * C,), dtype=jnp.float32) * 0.1
        phase_var = jax.random.uniform(ks[8], (2 * C,), jnp.float32, 0.5, 1.5)
        alpha = jnp.full((1,), 0.25, jnp.float32)
        return {'x': x, 'mag_w': mag_w, 'mag_b': mag_b, 'phase_w': phase_w, 'phase_b': phase_b, 'mag_gamma': mag_gamma, 'mag_beta': mag_beta, 'mag_mean': mag_mean, 'mag_var': mag_var, 'phase_gamma': phase_gamma, 'phase_beta': phase_beta, 'phase_mean': phase_mean, 'phase_var': phase_var, 'alpha': alpha}
    _L1_conv_all = _L1_conv_setup()
    _L1_conv_in = {k: v for k, v in _L1_conv_all.items() if k in ('mag_w', 'mag_b', 'phase_w', 'phase_b', 'mag_gamma', 'mag_beta', 'mag_mean', 'mag_var', 'phase_gamma', 'phase_beta', 'phase_mean', 'phase_var', 'alpha', )}
    del _L1_conv_all

    return {
        "x": x,
        "L0_conv_Wq": _L0_conv_in["Wq"],
        "L0_conv_Wk": _L0_conv_in["Wk"],
        "L0_conv_Wv": _L0_conv_in["Wv"],
        "L0_conv_Wo": _L0_conv_in["Wo"],
        "L0_conv_gamma": _L0_conv_in["gamma"],
        "L1_conv_mag_w": _L1_conv_in["mag_w"],
        "L1_conv_mag_b": _L1_conv_in["mag_b"],
        "L1_conv_phase_w": _L1_conv_in["phase_w"],
        "L1_conv_phase_b": _L1_conv_in["phase_b"],
        "L1_conv_mag_gamma": _L1_conv_in["mag_gamma"],
        "L1_conv_mag_beta": _L1_conv_in["mag_beta"],
        "L1_conv_mag_mean": _L1_conv_in["mag_mean"],
        "L1_conv_mag_var": _L1_conv_in["mag_var"],
        "L1_conv_phase_gamma": _L1_conv_in["phase_gamma"],
        "L1_conv_phase_beta": _L1_conv_in["phase_beta"],
        "L1_conv_phase_mean": _L1_conv_in["phase_mean"],
        "L1_conv_phase_var": _L1_conv_in["phase_var"],
        "L1_conv_alpha": _L1_conv_in["alpha"],
    }

def reference(x, L0_conv_Wq, L0_conv_Wk, L0_conv_Wv, L0_conv_Wo, L0_conv_gamma, L1_conv_mag_w, L1_conv_mag_b, L1_conv_phase_w, L1_conv_phase_b, L1_conv_mag_gamma, L1_conv_mag_beta, L1_conv_mag_mean, L1_conv_mag_var, L1_conv_phase_gamma, L1_conv_phase_beta, L1_conv_phase_mean, L1_conv_phase_var, L1_conv_alpha):
    import jax
    import jax.numpy as jnp
    def _L0_conv_ref(x, Wq, Wk, Wv, Wo, gamma):
        import jax, jax.numpy as jnp
        import numpy as np
        B, C, H, W = (4, 256, 64, 64)
        CQK = C // 8
        b, c, h, w = x.shape
        n = h * w
        xf = x.reshape(b, c, n)
        q = jnp.einsum('qc,bcn->bqn', Wq, xf)
        k = jnp.einsum('qc,bcn->bqn', Wk, xf)
        v = jnp.einsum('vc,bcn->bvn', Wv, xf)
        scale = 1.0 / jnp.sqrt(jnp.asarray(q.shape[1], dtype=x.dtype))
        attn = jnp.einsum('bqn,bqm->bnm', q, k) * scale
        attn = jax.nn.softmax(attn, axis=-1)
        out = jnp.einsum('bvm,bnm->bvn', v, attn)
        out = out.reshape(b, c, h, w)
        out = jnp.einsum('oc,bchw->bohw', Wo, out)
        return gamma[0] * out + x

    def _L1_conv_ref(x, mag_w, mag_b, phase_w, phase_b, mag_gamma, mag_beta, mag_mean, mag_var, phase_gamma, phase_beta, phase_mean, phase_var, alpha):
        import jax, jax.numpy as jnp
        import numpy as np
        EPS = 1e-05

        def _bn(x, gamma, beta, mean, var):
            scale = gamma * jax.lax.rsqrt(var + EPS)
            return (x - mean[:, None, None]) * scale[:, None, None] + beta[:, None, None]

        def _prelu(x, alpha):
            a = alpha[0]
            return jnp.where(x >= 0, x, a * x)

        def _up2_nearest(x):
            return jnp.repeat(jnp.repeat(x, 2, axis=2), 2, axis=3)
        B, C, H, W = x.shape
        ph, pw = (H // 8, W // 8)
        nP = ph * pw
        p = x.reshape(B, C, ph, 8, pw, 8).transpose(0, 2, 4, 1, 3, 5).reshape(B * nP, C, 8, 8)
        low = p.reshape(B * nP, C, 4, 2, 4, 2).mean(axis=(3, 5))
        high = p - _up2_nearest(low)
        low = jnp.einsum('oc,nchw->nohw', mag_w, low) + mag_b[:, None, None]
        low = _prelu(_bn(low, mag_gamma, mag_beta, mag_mean, mag_var), alpha)
        hs = jnp.concatenate([high, jnp.roll(high, 1, axis=2)], axis=1)
        hs = jnp.einsum('oc,nchw->nohw', phase_w, hs) + phase_b[:, None, None]
        hs = _prelu(_bn(hs, phase_gamma, phase_beta, phase_mean, phase_var), alpha)
        high = hs[:, :C]
        out = _up2_nearest(low) + high
        out = out.reshape(B, ph, pw, C, 8, 8).transpose(0, 3, 1, 4, 2, 5).reshape(B, C, H, W)
        return out

    def _gn(v, G=32, eps=1e-5):
        B_, C_, H_, W_ = v.shape
        g = v.reshape(B_, G, C_ // G, H_, W_)
        m = jnp.mean(g, axis=(2, 3, 4), keepdims=True)
        s = jnp.var(g, axis=(2, 3, 4), keepdims=True)
        return ((g - m) / jnp.sqrt(s + eps)).reshape(v.shape)

    def _ln_c(v, eps=1e-6):
        m = jnp.mean(v, axis=1, keepdims=True)
        s = jnp.var(v, axis=1, keepdims=True)
        return (v - m) / jnp.sqrt(s + eps)

    def _ln_t(v, eps=1e-5):
        m = jnp.mean(v, axis=-1, keepdims=True)
        s = jnp.var(v, axis=-1, keepdims=True)
        return (v - m) / jnp.sqrt(s + eps)

    def _to_tokens(v):
        B_, C_, H_, W_ = v.shape
        return v.reshape(B_, C_, H_ * W_).transpose(0, 2, 1)
    def _from_tokens(t, like):
        B_, C_, H_, W_ = like.shape
        return t.transpose(0, 2, 1).reshape(B_, C_, H_, W_)

    x = _L0_conv_ref(x, L0_conv_Wq, L0_conv_Wk, L0_conv_Wv, L0_conv_Wo, L0_conv_gamma)
    x = _L1_conv_ref(x, L1_conv_mag_w, L1_conv_mag_b, L1_conv_phase_w, L1_conv_phase_b, L1_conv_mag_gamma, L1_conv_mag_beta, L1_conv_mag_mean, L1_conv_mag_var, L1_conv_phase_gamma, L1_conv_phase_beta, L1_conv_phase_mean, L1_conv_phase_var, L1_conv_alpha)
    return x


_drawn_inputs = setup_inputs


def setup_inputs(seed=0):
    import zlib

    import numpy as np

    out = dict(_drawn_inputs(seed))
    spreads = {'L1_conv_mag_gamma': (1.0, 0.2),
     'L1_conv_mag_beta': (0.0, 0.1),
     'L1_conv_phase_gamma': (1.0, 0.2),
     'L1_conv_phase_beta': (0.0, 0.1)}
    factors = {'L1_conv_mag_b': 6.008, 'L1_conv_phase_b': 6.689}
    for name, (base, spread) in spreads.items():
        noise = np.random.default_rng([zlib.crc32(name.encode()), seed]).standard_normal(out[name].shape)
        drawn = base * np.exp(spread * noise) if base else spread * noise
        out[name] = jnp.asarray(drawn.astype(out[name].dtype))
    for name, factor in factors.items():
        out[name] = (out[name] * factor).astype(out[name].dtype)
    return out
```

```python
import concourse.bass as bass
from concourse import mybir
from contextlib import ExitStack

B, C, HW = 4, 256, 64 * 64
DQK = 32
CT = C // 128
CH = 512
NCH = HW // CH
MT = HW // 128
SUB = CH // 128
ALL = B * NCH
ROWS, WID = CH // 64, 64
LOWN = CH // 4
SCALE = DQK ** -0.5
EPS = 1e-5
SHIFT = 9.0
UW = C + 1
LEAD = 2

ROUND_A, ROUND_B, ROUND_CONV, NEGATIVE = 9, 11, 14, 25
DOUBLE = (9, 11, 13, 15, 17, 24, 27)
TASKS = {t: [] for t in range(MT)}
TASKS[0] += [("q",), ("k",)]
TASKS[2] += [("u", 0)]
TASKS[3] += [("u", 1)]
TASKS[6] += [("y", 0)]
TASKS[7] += [("y", 1)]
TASKS[19] += [("low",)]
TASKS[20] += [("high", 0)]
TASKS[22] += [("high", 1)]
MAXIMA = [(j, m) for j in range(SUB) for m in range(NCH)]
_left = list(MAXIMA)
for _t in range(4, 29):
    for _ in range(2 if _t in DOUBLE else 1):
        TASKS[_t].append(("max",) + _left.pop(0))
assert not _left
TASKS[29] += [("negmax",)]
NTASK = sum(len(v) for v in TASKS.values())
assert NTASK % 2 == 0
NUMBERED = {}
_n = 0
for _t in range(MT):
    NUMBERED[_t] = []
    for _task in TASKS[_t]:
        NUMBERED[_t].append((_n, _task))
        _n += 1
TAIL = [("y", 0), ("y", 1), ("low",), ("high", 0), ("high", 1)]
NUMBER = {task: n for tasks in NUMBERED.values() for n, task in tasks}
FIRST = [("wu", 0), ("wu", 1), ("q",)] + [("max",) + jm for jm in MAXIMA] + [("negmax",)]
assert len(FIRST) % 2 == 0 and NUMBER[("negmax",)] == NTASK - 1
A_FIRST, B_FIRST = 6, 5


def attention_conv(nc, x, wqk, wv, wo, phase_w, mag_w, params, gamma, alpha, out):
    f32, f32r, f16 = mybir.dt.float32, mybir.dt.float32r, mybir.dt.float16
    ALU, ACT, AX = mybir.AluOpType, mybir.ActivationFunctionType, mybir.AxisListType
    ds = bass.ds
    x_v = x.rearrange("b (t p) (k n) -> b k p t n", p=128, n=CH)
    out_v = out.rearrange("b (t p) (k n) -> b k p t n", p=128, n=CH)

    ctx = ExitStack()
    with ctx:
        def sb(name, shape, dt=f32):
            return ctx.enter_context(nc.sbuf_tensor(name, shape, dt))

        def sem(name):
            return ctx.enter_context(nc.semaphore(name))

        kst = sb("kst", [128, 2 * HW], f32r)
        uh = [sb(f"uh{i}", [128, MT, UW], f16) for i in range(2)]
        ul = [sb(f"ul{i}", [128, MT, C], f16) for i in range(2)]
        wq = [sb(f"wq{i}", [128, CT, 3 * DQK], f32r) for i in range(2)]
        wk = [sb(f"wk{i}", [128, CT, 3 * DQK], f32r) for i in range(2)]
        wu = [sb(f"wu{i}", [128, CT, C], f32r) for i in range(2)]
        wp = [sb(f"wp{i}", [128, 2 * CT, C], f32r) for i in range(2)]
        wm = [sb(f"wm{i}", [128, CT, C], f32r) for i in range(2)]
        ident = sb("ident", [128, 128])
        par = sb("par", [128, 5, 2, CT])
        var = sb("var", [128, 2, CT])
        half = sb("half", [128, 2, CT])
        spare = sb("spare", [128, 2])
        quarter = sb("quarter", [128, 1])
        rstd = sb("rstd", [128, 2, CT])
        bnA = sb("bnA", [128, 2, CT])
        bnB = sb("bnB", [128, 2, CT])
        al1 = sb("al1", [128, 1])
        gam = sb("gam", [128, 1])
        losel = sb("losel", [128, 1])
        amax = sb("amax", [128, B, NCH])
        bnd = sb("bnd", [128, 1 + CT])
        bndall = sb("bndall", [128, 1 + CT])
        prod = sb("prod", [128, 1])
        uscale = sb("uscale", [128, 1])
        ogain = sb("ogain", [128, 1])
        xa, xb, xr = sb("xa", [128, CT, CH]), sb("xb", [128, CT, CH]), sb("xr", [128, CT, CH])
        xah, xal = sb("xah", [128, CT, CH], f32r), sb("xal", [128, CT, CH], f32r)
        xbh, xbl = sb("xbh", [128, CT, CH], f32r), sb("xbl", [128, CT, CH], f32r)
        qst = sb("qst", [96, CH], f32r)
        qcur = sb("qcur", [128, CH], f32r)
        pmax = sb("pmax", [128, SUB, NCH])
        nmax = sb("nmax", [128, SUB])
        nhi = sb("nhi", [128, CH], f32r)
        p32 = sb("p32", [128, 2, CH])
        ph, pl = sb("ph", [128, 4, CH], f16), sb("pl", [128, 4, CH], f16)
        oraw = sb("oraw", [128, SUB, UW])
        rs = sb("rs", [128, SUB])
        on = sb("on", [128, SUB, C])
        y = sb("y", [128, CT, ROWS, WID])
        pair = sb("pair", [128, CT, ROWS, WID // 2])
        low4 = sb("low4", [128, CT, ROWS // 2, WID // 2])
        low = sb("low", [128, CT, LOWN])
        high = sb("high", [128, CT, ROWS, WID])
        hh, hl = [sb(n, [128, CT, ROWS + 1, WID], f32r) for n in ("hh", "hl")]
        lh, ll = [sb(n, [128, CT, LOWN], f32r) for n in ("lh", "ll")]
        zlow, zlneg = sb("zlow", [128, CT, LOWN]), sb("zlneg", [128, CT, LOWN])
        z, zneg = sb("z", [128, CT, CH]), sb("zneg", [128, CT, CH])
        wraw_p = z[:, :, :].rearrange("p t n -> p (t n)").rearrange("p (t n) -> p t n", n=C)
        wraw_m = zneg[:, 0, :].rearrange("p (t n) -> p t n", n=C)
        wraw_v = zneg[:, 1, :].rearrange("p (t n) -> p t n", n=C)
        wraw_o = on[:, 0:CT, :]
        wraw_qk = high[:, 0, 0:CT, :]
        scan = ul[1][:, :, :].rearrange("p m n -> p (m n)").bitcast(f32).rearrange("p (s t n) -> p s t n", s=B, t=CT)

        O = [ctx.enter_context(nc.psum_tensor(f"O{i}", [128, 512], f32)) for i in range(SUB)]
        S = [ctx.enter_context(nc.psum_tensor(f"S{i}", [128, 512], f32)) for i in range(2)]
        M = [ctx.enter_context(nc.psum_tensor(f"M{i}", [128, 512], f32)) for i in range(2)]
        PK = [[O[0], O[1], O[2]], [O[3], S[0], S[1]]]

        w_loaded, par_loaded = sem("w_loaded"), sem("par_loaded")
        scan_loaded, scanned = [sem(f"scan_loaded{b}") for b in range(B)], sem("scanned")
        xa_loaded, xb_loaded, xr_loaded = sem("xa_loaded"), sem("xb_loaded"), sem("xr_loaded")
        a_hi, b_hi = sem("a_hi"), sem("b_hi")
        a_split, b_split = sem("a_split"), sem("b_split")
        consts, pool_step = sem("consts"), sem("pool_step")
        w_hi, w_split, wu_hi = sem("w_hi"), sem("w_split"), sem("wu_hi")
        bound, reduced, scaled, dstep = sem("bound"), sem("reduced"), sem("scaled"), sem("dstep")
        var_ready, bn_ready = sem("var_ready"), sem("bn_ready")
        proj_filled, proj_hi, proj_free = sem("proj_filled"), sem("proj_hi"), sem("proj_free")
        m_filled = [sem("m0_filled"), sem("m1_filled")]
        m_free = [sem("m0_free"), sem("m1_free")]
        q_hi, k_hi, u_hi = sem("q_hi"), sem("k_hi"), sem("u_hi")
        nmax_ready, nhi_ready = sem("nmax_ready"), sem("nhi_ready")
        s_filled, probs_ready, lo_ready, pv_done = sem("s_filled"), sem("probs_ready"), sem("lo_ready"), sem("pv_done")
        o01_out, o23_out, rs_step, on_ready = sem("o01_out"), sem("o23_out"), sem("rs_step"), sem("on_ready")
        pairs_ready, low_ready, high_ready = sem("pairs_ready"), sem("low_ready"), sem("high_ready")
        hh_ready, conv_in = sem("hh_ready"), sem("conv_in")
        zneg_ready = sem("zneg_ready")
        prelu_ready, out_ready, out_stored = sem("prelu_ready"), sem("out_ready"), sem("out_stored")
        low4_ready, rstd_ready, banks_set, pmax_reduced = sem("low4_ready"), sem("rstd_ready"), sem("banks_set"), sem("pmax_reduced")

        FB = len(FIRST) // 2
        UB = NTASK // 2

        def use(g, n):
            return FB + UB * g + n // 2

        def emptied(eng, g, task):
            n = NUMBER[task] if g is not ALL else TAIL.index(task)
            eng.wait_ge(m_free[n % 2], use(g, n) + 1)

        def turns(eng, turn):
            with eng.Fori(0, B // 2) as pair_i:
                for parity in range(2):
                    with eng.Fori(0, NCH) as c:
                        turn(pair_i * (2 * NCH) + parity * NCH + c, parity, c)

        block = ctx.enter_context(nc.Block())

        @block.sync
        def _(sp):
            sp.dma_start(wraw_v, wv.rearrange("(t p) n -> p t n", p=128)).then_inc(w_loaded, 16)
            sp.dma_start(wraw_o, wo.rearrange("(t p) n -> p t n", p=128)).then_inc(w_loaded, 16)
            sp.dma_start(wraw_qk, wqk.rearrange("(t p) n -> p t n", p=128)).then_inc(w_loaded, 16)
            sp.dma_start(wraw_p, phase_w.rearrange("(t p) n -> p t n", p=128)).then_inc(w_loaded, 16)
            sp.dma_start(wraw_m, mag_w.rearrange("(t p) n -> p t n", p=128)).then_inc(w_loaded, 16)
            sp.dma_start(par[:, :, :, :], params).then_inc(par_loaded, 16)
            sp.dma_start(gam[:, :], gamma.partition_broadcast(128)).then_inc(par_loaded, 16)
            sp.dma_start(al1[:, :], alpha.partition_broadcast(128)).then_inc(par_loaded, 16)
            loads = [[(0, c) for c in (*range(0, NCH, 2), 0, 1)], [(0, c) for c in range(1, NCH, 2)] + [(1, 0)]]

            def load(i, buf, loaded, split, chunks):
                if i:
                    sp.wait_ge(split, i)
                sp.dma_start(buf[:, :, :], x_v[chunks[i]]).then_inc(loaded, 16)

            load(0, xa, xa_loaded, a_split, loads[0])
            load(0, xb, xb_loaded, b_split, loads[1])
            for b in range(B):
                sp.dma_start(scan[:, b, :, :], x_v[b, 0]).then_inc(scan_loaded[b], 16)
            with sp.Fori(1, NCH) as i:
                for b in range(B):
                    sp.wait_ge(scanned, B * i)
                    sp.dma_start(scan[:, b:b + 1, :, :], x_v[b:b + 1, ds(i, 1)].rearrange("b k p t n -> p (b k) t n")).then_inc(scan_loaded[b], 16)
            for i in range(1, A_FIRST):
                load(i, xa, xa_loaded, a_split, loads[0])
                if i < B_FIRST:
                    load(i, xb, xb_loaded, b_split, loads[1])
            sp.dma_start(xr[:, :, :], x_v[B - 1, NCH - 1]).then_inc(xr_loaded, 16)

            def turn(g, parity, c):
                sp.wait_ge(a_split, A_FIRST + g)
                gq = (g + 2) % ALL
                sp.dma_start(xa[:, :, :], x_v[ds(gq // NCH, 1), ds(gq % NCH, 1)]).then_inc(xa_loaded, 16)
                sp.wait_ge(b_split, B_FIRST + g)
                gk = (g + 1 + NCH) % ALL
                sp.dma_start(xb[:, :, :], x_v[ds(gk // NCH, 1), ds(gk % NCH, 1)]).then_inc(xb_loaded, 16)
                emptied(sp, g, ("y", 1))
                sp.dma_start(xr[:, :, :], x_v[ds(g // NCH, 1), ds(g % NCH, 1)]).then_inc(xr_loaded, 16)
                sp.wait_ge(out_ready, g + 2)
                gp = (g + (ALL - 1)) % ALL
                sp.dma_start(out_v[ds(gp // NCH, 1), ds(gp % NCH, 1)], z[:, :, :]).then_inc(out_stored, 16)

            turns(sp, turn)
            sp.wait_ge(out_ready, ALL + 2)
            sp.dma_start(out_v[B - 1, NCH - 1], z[:, :, :]).then_inc(out_stored, 16)
            sp.wait_ge(out_stored, 16 * (ALL + 2))
            sp.wait_ge(xa_loaded, 16 * (A_FIRST + ALL))
            sp.wait_ge(xb_loaded, 16 * (B_FIRST + ALL))

        @block.tensor
        def _(pe):
            def wide(bank, stat, mov, last=None):
                products = [(a, b) for pa, pb in ((0, 0), (0, 1), (1, 0)) for a, b in zip(stat[pa], mov[pb])]
                for i, (a, b) in enumerate(products):
                    ins = nc.tensor.matmul(bank, a, b, start=(i == 0), stop=(i == len(products) - 1))
                return ins

            def project_rows(bank, w, xs):
                return wide(bank[0:3 * DQK, :], [[w[v][:, t, :] for t in range(CT)] for v in range(2)],
                            [[xs[v][:, t, :] for t in range(CT)] for v in range(2)])

            def project_u(bank, xs, half_i):
                for m in range(2):
                    px = slice((2 * half_i + m) * 128, (2 * half_i + m + 1) * 128)
                    ins = wide(bank[:, m * C:(m + 1) * C], [[xs[v][:, t, px] for t in range(CT)] for v in range(2)],
                               [[wu[v][:, t, :] for t in range(CT)] for v in range(2)])
                return ins

            def project(bank, kind, hf, xs):
                if kind == "u":
                    return project_u(bank, xs, hf)
                return project_rows(bank, wk if kind == "k" else wq, xs)

            def transposed(bank, h):
                for j in range(SUB):
                    ins = nc.tensor.transpose(bank[:, j * 128:(j + 1) * 128], on[:, j, h * 128:(h + 1) * 128], ident[:, :])
                return ins

            def low_conv(bank):
                for o in range(CT):
                    ins = wide(bank[:, o * LOWN:(o + 1) * LOWN],
                               [[wm[v][:, t, o * 128:(o + 1) * 128] for t in range(CT)] for v in range(2)],
                               [[(lh, ll)[v][:, t, :] for t in range(CT)] for v in range(2)])
                return ins

            def high_conv(bank, oh):
                return wide(bank[:, :], [[wp[v][:, s * CT + t, oh * 128:(oh + 1) * 128] for s in range(2) for t in range(CT)]
                                         for v in range(2)],
                            [[(hh, hl)[v][:, t, 1 - s:1 - s + ROWS, :].rearrange("p r w -> p (r w)")
                              for s in range(2) for t in range(CT)] for v in range(2)])

            def max_scores(bank, j, keys_at):
                return nc.tensor.matmul(bank[:, :], qst[:, j * 128:(j + 1) * 128], kst[0:96, keys_at],
                                        start=True, stop=True)

            def negmax_rows(bank):
                for j in range(SUB):
                    ins = nc.tensor.transpose(bank[:, j * 128:(j + 1) * 128],
                                              nmax[:, j:j + 1].to_broadcast([128, 128]), ident[:, :])
                return ins

            pe.wait_ge(w_loaded, 5 * 16)
            pe.wait_ge(consts, 1)
            for n in range(2):
                for t in range(CT):
                    ins = nc.tensor.matmul(M[n][:, 0:C], wraw_v[:, t, n * 128:(n + 1) * 128],
                                           wraw_o[:, t, :], start=(t == 0), stop=(t == CT - 1))
                ins.then_inc(m_filled[n], 1)
            nc.tensor.transpose(O[0][:, 0:128], ident[:, :], ident[:, :]).then_inc(pv_done, 1)
            pe.wait_ge(w_split, 1)
            for n in range(CT):
                pe.wait_ge(m_free[n], 1)
            with pe.Fori(0, NCH // 2) as i:
                for s, xs, split in ((0, (xah, xal), a_split), (1, (xbh, xbl), b_split)):
                    pe.wait_ge(split, i + 1)
                    pe.wait_ge(proj_free, 6 * i + 3 * s + 1)
                    project_rows(PK[s][0], wk, xs).then_inc(proj_filled, 1)
                    for hf in range(2):
                        project_u(PK[s][1 + hf], xs, hf).then_inc(proj_filled, 1)
            pe.wait_ge(a_split, A_FIRST - 1)
            for n in range(2, len(FIRST)):
                kind = FIRST[n][0]
                pe.wait_ge(m_free[n % 2], n // 2)
                if kind == "q":
                    project(M[n % 2], "q", 0, (xah, xal)).then_inc(m_filled[n % 2], 1)
                elif kind == "max":
                    _, j, m = FIRST[n]
                    if (j, m) == MAXIMA[0]:
                        pe.wait_ge(m_free[0], 2)
                        pe.wait_ge(proj_free, 4 + 3 * NCH)
                    max_scores(M[n % 2], j, slice(m * CH, (m + 1) * CH)).then_inc(m_filled[n % 2], 1)
                else:
                    pe.wait_ge(nmax_ready, 1)
                    negmax_rows(M[n % 2]).then_inc(m_filled[n % 2], 1)

            def scores(g, parity, t):
                if t >= LEAD:
                    pe.wait_ge(probs_ready, MT * g + t - 1)
                at = parity * HW + t * 128
                nc.tensor.matmul(S[t % 2][:, :], kst[:, at:at + 128], qcur[:, :],
                                 start=True, stop=True).then_inc(s_filled, 1)

            def tasks(g, keys_next, t):
                for n, task in NUMBERED[t]:
                    kind = task[0]
                    bank = M[n % 2]
                    pe.wait_ge(m_free[n % 2], use(g, n))
                    if kind == "q":
                        pe.wait_ge(a_split, A_FIRST + g)
                        ins = project(bank, "q", 0, (xah, xal))
                    elif kind in ("k", "u"):
                        pe.wait_ge(b_split, B_FIRST + g)
                        ins = project(bank, kind, task[-1], (xbh, xbl))
                    elif kind == "y":
                        pe.wait_ge(on_ready, g + 2)
                        ins = transposed(bank, task[1])
                    elif kind == "low":
                        pe.wait_ge(conv_in, g + 1)
                        ins = low_conv(bank)
                    elif kind == "high":
                        ins = high_conv(bank, task[1])
                    elif kind == "max":
                        _, j, m = task
                        if (j, m) == MAXIMA[0]:
                            emptied(pe, g, ("q",))
                            emptied(pe, g, ("k",))
                        ins = max_scores(bank, j, ds(keys_next + m * CH, CH))
                    else:
                        pe.wait_ge(nmax_ready, g + 2)
                        ins = negmax_rows(bank)
                    ins.then_inc(m_filled[n % 2], 1)

            def weigh(g, parity, t):
                pe.wait_ge(lo_ready, MT * g + t + 1)
                for j in range(SUB):
                    if t == 0:
                        pe.wait_ge((o01_out, o23_out)[j // 2], 2 * g + j % 2 + 1)
                    q = slice(j * 128, (j + 1) * 128)
                    nc.tensor.matmul(O[j][:, 0:UW], ph[:, t % 4, q], uh[parity][:, t, :], start=(t == 0), stop=False)
                    nc.tensor.matmul(O[j][:, 0:C], ph[:, t % 4, q], ul[parity][:, t, :], start=False, stop=False)
                    ins = nc.tensor.matmul(O[j][:, 0:UW], pl[:, t % 4, q], uh[parity][:, t, :],
                                           start=False, stop=(t == MT - 1))
                ins.then_inc(pv_done, 1)

            def turn(g, parity, c):
                keys_next = pe.snap(((c + (parity * NCH + 1)) // NCH) % 2 * HW)
                pe.wait_ge(m_free[1], use(g, 0))
                for t in range(LEAD):
                    scores(g, parity, t)
                for t in range(MT):
                    if t == 0:
                        tasks(g, keys_next, t)
                    if t + LEAD < MT:
                        scores(g, parity, t + LEAD)
                    if t > 0:
                        tasks(g, keys_next, t)
                    weigh(g, parity, t)

            turns(pe, turn)
            for n, task in enumerate(TAIL):
                pe.wait_ge(m_free[n % 2], use(ALL, n))
                if task[0] == "y":
                    pe.wait_ge(on_ready, ALL + 2)
                    ins = transposed(M[n % 2], task[1])
                elif task[0] == "low":
                    pe.wait_ge(conv_in, ALL + 1)
                    ins = low_conv(M[n % 2])
                else:
                    ins = high_conv(M[n % 2], task[1])
                ins.then_inc(m_filled[n % 2], 1)

        @block.scalar
        def _(act):
            def round_x(xs, hi, loaded, count, ready):
                act.wait_ge(loaded, count * 16)
                nc.scalar.activation(hi[:, :, :], xs[:, :, :], ACT.Copy).then_inc(ready, 1)

            act.wait_ge(w_loaded, 5 * 16)
            for s in range(3):
                nc.scalar.activation(wq[0][:, :, s * DQK:(s + 1) * DQK], wraw_qk[:, :, 0:DQK], ACT.Copy)
                nc.scalar.activation(wk[0][:, :, s * DQK:(s + 1) * DQK], wraw_qk[:, :, DQK:2 * DQK], ACT.Copy)
            nc.scalar.activation(wp[0][:, :, :], wraw_p, ACT.Copy)
            nc.scalar.activation(wm[0][:, :, :], wraw_m, ACT.Copy).then_inc(w_hi, 1)
            for n in range(CT):
                act.wait_ge(m_filled[n], 1)
                nc.scalar.activation(wu[0][:, n, :], M[n][:, 0:C], ACT.Copy).then_inc(wu_hi, 1)
            round_x(xa, xah, xa_loaded, 1, a_hi)
            round_x(xb, xbh, xb_loaded, 1, b_hi)
            act.wait_ge(scaled, 1)
            with act.Fori(0, NCH // 2) as i:
                for s, xs, hi, loaded, ready in ((0, xa, xah, xa_loaded, a_hi), (1, xb, xbh, xb_loaded, b_hi)):
                    filled = 6 * i + 3 * s
                    act.wait_ge(proj_filled, filled + 1)
                    nc.scalar.activation(kst[0:96, ds((2 * i + s) * CH, CH)], PK[s][0][0:96, :], ACT.Copy).then_inc(proj_hi, 1)
                    for hf in range(2):
                        act.wait_ge(proj_filled, filled + 2 + hf)
                        nc.scalar.activation(uh[0][:, ds((2 * i + s) * SUB + 2 * hf, 2), 0:C],
                                             PK[s][1 + hf][:, :].rearrange("p (m n) -> p m n", n=C),
                                             ACT.Copy, scale=uscale[:, 0:1]).then_inc(proj_hi, 1)
                    act.wait_ge(loaded, (i + 2) * 16)
                    nc.scalar.activation(hi[:, :, :], xs[:, :, :], ACT.Copy).then_inc(ready, 1)
            act.wait_ge(m_filled[0], 2)
            nc.scalar.activation(qst[:, :], M[0][0:96, :], ACT.Copy).then_inc(q_hi, 1)
            round_x(xa, xah, xa_loaded, A_FIRST, a_hi)
            act.wait_ge(bn_ready, 1)
            act.wait_ge(banks_set, 1)

            def copy_out(g, j):
                act.wait_ge(pv_done, MT * g + 1)
                act.wait_ge(on_ready, g + 1)
                nc.scalar.activation(oraw[:, j, :], O[j][:, 0:UW], ACT.Copy).then_inc(o01_out, 1)

            def probabilities(g, t):
                act.wait_ge(s_filled, MT * g + t + 1)
                if t >= 4:
                    act.wait_ge(pv_done, MT * g + t - 2)
                nc.scalar.activation(ph[:, t % 4, :], S[t % 2][:, :], ACT.Exp, scale=SCALE)
                if t >= 2:
                    act.wait_ge(lo_ready, MT * g + t - 1)
                nc.scalar.activation(p32[:, t % 2, :], S[t % 2][:, :], ACT.Exp, scale=SCALE).then_inc(probs_ready, 1)

            def take(bank, task, g, parity, c):
                kind = task[0]
                if kind == "q":
                    act.wait_ge(m_free[1], use(g, 0))
                    nc.scalar.activation(qst[:, :], bank[0:96, :], ACT.Copy).then_inc(q_hi, 1)
                elif kind == "k":
                    nc.scalar.activation(kst[0:96, ds(c * CH + (1 - parity) * HW, CH)], bank[0:96, :], ACT.Copy).then_inc(k_hi, 1)
                elif kind == "u":
                    nc.scalar.activation(uh[1 - parity][:, ds(c * SUB + 2 * task[1], 2), 0:C],
                                         bank[:, :].rearrange("p (m n) -> p m n", n=C),
                                         ACT.Copy, scale=uscale[:, 0:1]).then_inc(u_hi, 1)

            def norm_low(bank, g, free):
                act.wait_ge(out_ready, g + 1)
                for o in range(CT):
                    ins = nc.scalar.activation(zlow[:, o, :], bank[:, o * LOWN:(o + 1) * LOWN], ACT.Identity,
                                               scale=bnA[:, 0, o:o + 1], bias=bnB[:, 0, o:o + 1])
                ins.then_inc(free, 1)

            def norm_high(bank, g, o, free):
                act.wait_ge(out_stored, 16 * g + 16)
                nc.scalar.activation(z[:, o, :], bank[:, :], ACT.Identity, scale=bnA[:, 1, o:o + 1],
                                     bias=bnB[:, 1, o:o + 1]).then_inc(free, 1)

            def round_conv(g):
                act.wait_ge(high_ready, g + 2)
                nc.scalar.activation(hh[:, :, 1:ROWS + 1, :], high[:, :, :, :], ACT.Copy)
                nc.scalar.activation(hh[:, :, 0, :], high[:, :, ROWS - 1, :], ACT.Copy)
                nc.scalar.activation(lh[:, :, :], low[:, :, :], ACT.Copy).then_inc(hh_ready, 1)

            def turn(g, parity, c):
                copy_out(g, 0)
                probabilities(g, 0)
                copy_out(g, 1)
                probabilities(g, 1)
                for t in range(MT):
                    if 0 < t < MT - LEAD:
                        probabilities(g, t + LEAD)
                    for n, task in NUMBERED[t]:
                        bank = M[n % 2]
                        if task[0] in ("q", "k", "u", "low", "high"):
                            act.wait_ge(m_filled[n % 2], use(g, n) + 1)
                        if task[0] == "low":
                            norm_low(bank, g, m_free[n % 2])
                        elif task[0] == "high":
                            norm_high(bank, g, task[1], m_free[n % 2])
                        else:
                            take(bank, task, g, parity, c)
                    if t == 0:
                        probabilities(g, LEAD)
                    if t == ROUND_A:
                        act.wait_ge(xa_loaded, (g + A_FIRST + 1) * 16)
                        nc.scalar.activation(xah[:, :, :], xa[:, :, :], ACT.Copy).then_inc(a_hi, 1)
                    if t == ROUND_B:
                        act.wait_ge(xb_loaded, (g + B_FIRST + 1) * 16)
                        nc.scalar.activation(xbh[:, :, :], xb[:, :, :], ACT.Copy).then_inc(b_hi, 1)
                    if t == ROUND_CONV:
                        round_conv(g)

            turns(act, turn)
            copy_out(ALL, 0)
            copy_out(ALL, 1)
            round_conv(ALL)
            for n, task in enumerate(TAIL):
                if task[0] != "y":
                    act.wait_ge(m_filled[n % 2], use(ALL, n) + 1)
                    if task[0] == "low":
                        norm_low(M[n % 2], ALL, m_free[n % 2])
                    else:
                        norm_high(M[n % 2], ALL, task[1], m_free[n % 2])

        @block.vector
        def _(dve):
            chain = [0]

            def done(ins):
                chain[0] += 1
                ins.then_inc(dstep, 1)
                dve.wait_ge(dstep, chain[0])

            nc.vector.memset(half[:, :, :], -0.5).then_inc(on_ready, 1)
            nc.vector.memset(quarter[:, :], 0.25).then_inc(out_stored, 16)
            for i in range(2):
                nc.vector.memset(uh[i][:, :, C:C + 1], 1.0)
            dve.wait_ge(par_loaded, 3 * 16)
            done(nc.vector.tensor_scalar(var[:, :, :], par[:, 4, :, :], EPS, None, ALU.add))
            nc.vector.tensor_scalar(al1[:, :], al1[:, :], 1.0, None, ALU.subtract).then_inc(var_ready, 1)
            dve.wait_ge(consts, 1)
            done(nc.vector.tensor_tensor(prod[:, :], ident[:, 96:97], ident[:, 97:98], ALU.add))
            nc.vector.tensor_scalar(kst[96:128, :], ident[96:128, 0:1].to_broadcast([32, 2 * HW]), 0.0,
                                    prod[96:128, 0:1], ALU.mult, ALU.add)
            done(nc.vector.tensor_scalar(losel[:, :], ident[:, 96:97], 1.0, None, ALU.subtract))
            dve.wait_ge(rstd_ready, 1)
            done(nc.vector.tensor_tensor(bnA[:, :, :], par[:, 1, :, :], rstd[:, :, :], ALU.mult))
            done(nc.vector.tensor_tensor(bnB[:, :, :], par[:, 0, :, :], par[:, 3, :, :], ALU.subtract))
            done(nc.vector.tensor_tensor(bnB[:, :, :], bnB[:, :, :], bnA[:, :, :], ALU.mult))
            nc.vector.tensor_tensor(bnB[:, :, :], bnB[:, :, :], par[:, 2, :, :], ALU.add).then_inc(bn_ready, 1)
            dve.wait_ge(w_hi, 1)
            for s in range(3):
                cols = slice(s * DQK, (s + 1) * DQK)
                for w, raw in ((wq, wraw_qk[:, :, 0:DQK]), (wk, wraw_qk[:, :, DQK:2 * DQK])):
                    nc.vector.tensor_tensor(w[1][:, :, cols], raw, w[0][:, :, cols].bitcast(f32), ALU.subtract)
            nc.vector.tensor_tensor(wp[1][:, :, :], wraw_p, wp[0][:, :, :].bitcast(f32), ALU.subtract)
            nc.vector.tensor_tensor(wm[1][:, :, :], wraw_m, wm[0][:, :, :].bitcast(f32), ALU.subtract).then_inc(w_split, 1)
            for n in range(CT):
                dve.wait_ge(wu_hi, n + 1)
                nc.vector.tensor_reduce(bnd[:, 1 + n:2 + n], M[n][:, 0:C], AX.X, ALU.max, apply_absolute_value=True)
                nc.vector.tensor_tensor(wu[1][:, n, :], M[n][:, 0:C], wu[0][:, n, :].bitcast(f32),
                                        ALU.subtract).then_inc(m_free[n], 1)

            def split_x(xs, hi, lo, rounded, count, ready):
                dve.wait_ge(rounded, count)
                nc.vector.tensor_tensor(lo[:, :, :], xs[:, :, :], hi[:, :, :].bitcast(f32), ALU.subtract).then_inc(ready, 1)

            split_x(xa, xah, xal, a_hi, 1, a_split)
            split_x(xb, xbh, xbl, b_hi, 1, b_split)
            with dve.Fori(0, NCH) as i:
                for b in range(B):
                    dve.wait_ge(scan_loaded[b], (i + 1) * 16)
                    nc.vector.tensor_reduce(amax[:, b, ds(i, 1)], scan[:, b, :, :].rearrange("p t n -> p (t n)"),
                                            AX.X, ALU.max, apply_absolute_value=True).then_inc(scanned, 1)
            dve.wait_ge(scanned, ALL)
            nc.vector.tensor_reduce(bnd[:, 0:1], amax[:, :, :].rearrange("p b k -> p (b k)"), AX.X, ALU.max).then_inc(bound, 1)
            dve.wait_ge(reduced, 1)
            done(nc.vector.tensor_tensor(prod[:, :], bndall[:, 1:2], bndall[:, 2:3], ALU.max))
            done(nc.vector.tensor_tensor(prod[:, :], prod[:, :], bndall[:, 0:1], ALU.mult))
            done(nc.vector.tensor_scalar(prod[:, :], prod[:, :], C / 2.0 ** 15, 1e-30, ALU.mult, ALU.max))
            nc.vector.reciprocal(uscale[:, :], prod[:, :]).then_inc(scaled, 1)
            nc.vector.tensor_tensor(ogain[:, :], prod[:, :], gam[:, :], ALU.mult).then_inc(proj_free, 4)
            with dve.Fori(0, NCH // 2) as i:
                for s, xs, hi, lo, rounded, ready in ((0, xa, xah, xal, a_hi, a_split), (1, xb, xbh, xbl, b_hi, b_split)):
                    filled = 6 * i + 3 * s
                    dve.wait_ge(proj_hi, filled + 1)
                    keys = kst[32:64, ds((2 * i + s) * CH, CH)]
                    nc.vector.tensor_tensor(keys, PK[s][0][32:64, :], keys.bitcast(f32), ALU.subtract).then_inc(proj_free, 1)
                    for hf in range(2):
                        dve.wait_ge(proj_hi, filled + 2 + hf)
                        tiles = ds((2 * i + s) * SUB + 2 * hf, 2)
                        nc.vector.scalar_tensor_tensor(ul[0][:, tiles, :], PK[s][1 + hf][:, :].rearrange("p (m n) -> p m n", n=C),
                                                       uscale[:, 0:1], uh[0][:, tiles, 0:C], ALU.mult, ALU.subtract)\
                            .then_inc(proj_free, 1)
                    dve.wait_ge(rounded, i + 2)
                    nc.vector.tensor_tensor(lo[:, :, :], xs[:, :, :], hi[:, :, :].bitcast(f32), ALU.subtract).then_inc(ready, 1)
            dve.wait_ge(proj_free, 4 + 3 * NCH)
            for j in range(SUB):
                ins = nc.vector.memset(O[j][:, :], 1.0)
            ins.then_inc(banks_set, 1)

            def low_q(bank, count, free):
                dve.wait_ge(q_hi, count)
                nc.vector.tensor_tensor(qst[64:96, :], bank[64:96, :], qst[64:96, :].bitcast(f32),
                                        ALU.subtract).then_inc(free, 1)

            def partial_max(bank, j, m, free):
                nc.vector.tensor_reduce(pmax[:, j, m:m + 1], bank[:, :], AX.X, ALU.max).then_inc(free, 1)

            def maxima(count):
                nc.vector.tensor_reduce(nmax[:, :], pmax[:, :, :], AX.X, ALU.max, negate=True).then_inc(pmax_reduced, 1)
                dve.wait_ge(pmax_reduced, count)
                nc.vector.tensor_scalar(nmax[:, :], nmax[:, :], SHIFT / SCALE, None, ALU.add).then_inc(nmax_ready, 1)

            def finish_q(bank, count, free):
                dve.wait_ge(nhi_ready, count)
                nc.vector.tensor_copy(qcur[0:96, :], qst[:, :].bitcast(f32))
                nc.vector.scalar_tensor_tensor(qcur[96:128, :], nhi[96:128, :].bitcast(f32), losel[96:128, 0:1],
                                               bank[96:128, :], ALU.mult, ALU.add).then_inc(free, 1)

            for n in range(2, len(FIRST)):
                kind, bank, free = FIRST[n][0], M[n % 2], m_free[n % 2]
                if kind == "q":
                    low_q(bank, 1, free)
                    split_x(xa, xah, xal, a_hi, A_FIRST, a_split)
                    continue
                dve.wait_ge(m_filled[n % 2], n // 2 + 1)
                if kind == "max":
                    partial_max(bank, *FIRST[n][1:], free)
                    if FIRST[n][1:] == MAXIMA[-1]:
                        dve.wait_ge(free, n // 2 + 1)
                        maxima(1)
                else:
                    nc.vector.tensor_copy(nhi[96:128, :], bank[96:128, :]).then_inc(nhi_ready, 1)
                    finish_q(bank, 1, free)

            def copy_out(g, j):
                dve.wait_ge(pv_done, MT * g + 1)
                dve.wait_ge(on_ready, g + 1)
                nc.vector.tensor_copy(oraw[:, j, :], O[j][:, 0:UW]).then_inc(o23_out, 1)

            def normalise(g):
                dve.wait_ge(o01_out, 2 * g + 2)
                dve.wait_ge(o23_out, 2 * g + 2)
                nc.vector.reciprocal(rs[:, :], oraw[:, :, C]).then_inc(rs_step, 1)
                dve.wait_ge(rs_step, 2 * g + 1)
                nc.vector.tensor_scalar(rs[:, :], rs[:, :], ogain[:, 0:1], None, ALU.mult).then_inc(rs_step, 1)
                dve.wait_ge(rs_step, 2 * g + 2)
                for j in range(SUB):
                    ins = nc.vector.tensor_scalar(on[:, j, :], oraw[:, j, 0:C], rs[:, j:j + 1], None, ALU.mult)
                ins.then_inc(on_ready, 1)

            def low_probabilities(g, t):
                dve.wait_ge(probs_ready, MT * g + t + 1)
                nc.vector.tensor_tensor(pl[:, t % 4, :], p32[:, t % 2, :], ph[:, t % 4, :], ALU.subtract).then_inc(lo_ready, 1)

            def add_residual(bank, g, h, free):
                if h == 0:
                    dve.wait_ge(xr_loaded, 16 * g + 16)
                    dve.wait_ge(high_ready, g + 1)
                nc.vector.tensor_tensor(y[:, h, :, :].rearrange("p r w -> p (r w)"), bank[:, :], xr[:, h, :],
                                        ALU.add).then_inc(free, 1)

            def negative_parts(g):
                emptied(dve, g, ("low",))
                nc.vector.tensor_scalar(zlneg[:, :, :], zlow[:, :, :], 0.0, al1[:, 0:1], ALU.min, ALU.mult)
                emptied(dve, g, ("high", 0))
                emptied(dve, g, ("high", 1))
                nc.vector.tensor_scalar(zneg[:, :, :], z[:, :, :], 0.0, al1[:, 0:1], ALU.min, ALU.mult).then_inc(zneg_ready, 1)

            def take(n, task, g, parity, c):
                kind, bank, free = task[0], M[n % 2], m_free[n % 2]
                if kind == "q":
                    low_q(bank, g + 2, free)
                elif kind == "k":
                    dve.wait_ge(k_hi, g + 1)
                    keys = kst[32:64, ds(c * CH + (1 - parity) * HW, CH)]
                    nc.vector.tensor_tensor(keys, bank[32:64, :], keys.bitcast(f32),
                                            ALU.subtract).then_inc(free, 1)
                elif kind == "u":
                    dve.wait_ge(u_hi, 2 * g + 1 + task[1])
                    tiles = ds(c * SUB + 2 * task[1], 2)
                    nc.vector.scalar_tensor_tensor(ul[1 - parity][:, tiles, :], bank[:, :].rearrange("p (m n) -> p m n", n=C),
                                                   uscale[:, 0:1], uh[1 - parity][:, tiles, 0:C], ALU.mult, ALU.subtract)\
                        .then_inc(free, 1)
                elif kind in ("y", "max", "negmax"):
                    dve.wait_ge(m_filled[n % 2], use(g, n) + 1)
                    if kind == "y":
                        add_residual(bank, g, task[1], free)
                    elif kind == "max":
                        partial_max(bank, task[1], task[2], free)
                        if task[1:] == MAXIMA[-1]:
                            emptied(dve, g, task)
                            maxima(g + 2)
                    else:
                        nc.vector.tensor_copy(nhi[96:128, :], bank[96:128, :]).then_inc(nhi_ready, 1)

            def turn(g, parity, c):
                copy_out(g, 2)
                copy_out(g, 3)
                low_probabilities(g, 0)
                for t in range(MT):
                    if t + 1 < MT:
                        low_probabilities(g, t + 1)
                    if t == 0:
                        normalise(g)
                    for n, task in NUMBERED[t]:
                        take(n, task, g, parity, c)
                    if t == NEGATIVE:
                        negative_parts(g)
                dve.wait_ge(s_filled, MT * g + MT)
                finish_q(M[(NTASK - 1) % 2], g + 2, m_free[(NTASK - 1) % 2])

            turns(dve, turn)
            copy_out(ALL, 2)
            copy_out(ALL, 3)
            normalise(ALL)
            for n, task in enumerate(TAIL[:CT]):
                dve.wait_ge(m_filled[n % 2], use(ALL, n) + 1)
                add_residual(M[n % 2], ALL, task[1], m_free[n % 2])
            negative_parts(ALL)

        @block.gpsimd
        def _(pool):
            nc.gpsimd.memset(ident[:, :], 0.0).then_inc(pool_step, 1)
            pool.wait_ge(pool_step, 1)
            nc.gpsimd.affine_select(out=ident[:, :], in_=ident[:, :], compare_op=ALU.not_equal, fill=1.0, base=0,
                                    pattern=[[-1, 128]], channel_multiplier=1).then_inc(consts, 1)
            nc.gpsimd.memset(spare[:, 0:1], 0.0).then_inc(out_ready, 1)
            nc.gpsimd.memset(spare[:, 1:2], 0.0).then_inc(high_ready, 1)
            pool.wait_ge(var_ready, 1)
            nc.gpsimd.tensor_tensor(rstd[:, :, :], var[:, :, :], half[:, :, :], ALU.pow).then_inc(rstd_ready, 1)
            pool.wait_ge(bound, 1)
            nc.gpsimd.partition_all_reduce(bndall[:, :], bnd[:, :], 128, bass.bass_isa.ReduceOp.max).then_inc(reduced, 1)

            HR = ROWS // 2

            def rows(buf, t, r):
                return buf[:, t, :, :].rearrange("p (h two) (w s) -> p two h w s", two=2, s=2)[:, r]

            def spread(buf, t):
                return buf[:, t, :].rearrange("p (h w a) -> p h w a", h=HR, a=1).to_broadcast([128, HR, WID // 2, 2])

            def split_frequencies(g):
                emptied(pool, g, ("y", 1))
                for t in range(CT):
                    yp = y[:, t, :, :].rearrange("p r (w s) -> p s r w", s=2)
                    ins = nc.gpsimd.tensor_tensor(pair[:, t, :, :], yp[:, 0], yp[:, 1], ALU.add)
                ins.then_inc(pairs_ready, 1)
                pool.wait_ge(pairs_ready, g + 1)
                pp = pair[:, :, :, :].rearrange("p t (h s) w -> p s (t h) w", s=2)
                nc.gpsimd.tensor_tensor(low4[:, :, :, :].rearrange("p t h w -> p (t h) w"), pp[:, 0], pp[:, 1],
                                        ALU.add).then_inc(low4_ready, 1)
                pool.wait_ge(low4_ready, g + 1)
                nc.gpsimd.tensor_tensor(low[:, :, :].rearrange("p t n -> p (t n)"),
                                        low4[:, :, :, :].rearrange("p t h w -> p (t h w)"),
                                        quarter[:, 0:1].to_broadcast([128, CT * LOWN]), ALU.mult).then_inc(low_ready, 1)
                pool.wait_ge(low_ready, g + 1)
                for t in range(CT):
                    for r in range(2):
                        ins = nc.gpsimd.tensor_tensor(rows(high, t, r), rows(y, t, r), spread(low, t), ALU.subtract)
                ins.then_inc(high_ready, 1)

            def low_x(xs, hi, lo, rounded, count, ready):
                pool.wait_ge(rounded, count)
                for t in range(CT):
                    for px in (slice(0, CH // 2), slice(CH // 2, CH)):
                        ins = nc.gpsimd.tensor_tensor(lo[:, t, px], xs[:, t, px], hi[:, t, px].bitcast(f32), ALU.subtract)
                ins.then_inc(ready, 1)

            def low_conv_in(g):
                pool.wait_ge(hh_ready, g + 1)
                for t in range(CT):
                    for r in (0, HR):
                        nc.gpsimd.tensor_tensor(hl[:, t, 1 + r:1 + r + HR, :], high[:, t, r:r + HR, :],
                                                hh[:, t, 1 + r:1 + r + HR, :].bitcast(f32), ALU.subtract)
                nc.gpsimd.tensor_tensor(hl[:, :, 0, :], high[:, :, ROWS - 1, :], hh[:, :, 0, :].bitcast(f32), ALU.subtract)
                nc.gpsimd.tensor_tensor(ll[:, :, :], low[:, :, :], lh[:, :, :].bitcast(f32), ALU.subtract).then_inc(conv_in, 1)

            def add_up(g):
                pool.wait_ge(zneg_ready, g + 1)
                nc.gpsimd.tensor_tensor(zlow[:, :, :], zlow[:, :, :], zlneg[:, :, :], ALU.add)
                for t in range(CT):
                    for px in (slice(0, CH // 2), slice(CH // 2, CH)):
                        ins = nc.gpsimd.tensor_tensor(z[:, t, px], z[:, t, px], zneg[:, t, px], ALU.add)
                ins.then_inc(prelu_ready, 1)
                pool.wait_ge(prelu_ready, g + 1)
                for t in range(CT):
                    zr = z[:, t, :].rearrange("p (h two w s) -> p two h w s", h=HR, two=2, s=2)
                    for r in range(2):
                        ins = nc.gpsimd.tensor_tensor(zr[:, r], zr[:, r], spread(zlow, t), ALU.add)
                ins.then_inc(out_ready, 1)

            def turn(g, parity, c):
                split_frequencies(g)
                low_x(xa, xah, xal, a_hi, g + A_FIRST + 1, a_split)
                low_x(xb, xbh, xbl, b_hi, g + B_FIRST + 1, b_split)
                low_conv_in(g)
                add_up(g)

            turns(pool, turn)
            split_frequencies(ALL)
            low_conv_in(ALL)
            add_up(ALL)


def kernel(**inputs):
    import numpy as np
    import concourse.bacc as bacc
    from concourse.bass_utils import run_bass_kernel_spmd

    a = {k: np.asarray(v) for k, v in inputs.items()}
    both = [[a[f"L1_conv_{kind}_{p}"][:C] for kind in ("mag", "phase")] for p in ("b", "gamma", "beta", "mean", "var")]
    laid = {
        "x": a["x"].reshape(B, C, HW),
        "wqk": np.concatenate([a["L0_conv_Wq"], a["L0_conv_Wk"]]).T,
        "wv": a["L0_conv_Wv"],
        "wo": a["L0_conv_Wo"].T,
        "phase_w": a["L1_conv_phase_w"][:C].T,
        "mag_w": a["L1_conv_mag_w"].T,
        "params": np.stack([np.stack(p) for p in both]).reshape(5, 2, CT, 128).transpose(3, 0, 1, 2),
        "gamma": a["L0_conv_gamma"],
        "alpha": a["L1_conv_alpha"],
    }
    nc = bacc.Bacc("TRN2", target_bir_lowering=False, num_devices=1)
    arrays, args = {}, []
    for name, v in laid.items():
        v = np.ascontiguousarray(v)
        arrays[f"in_{name}"] = v
        args.append(nc.dram_tensor(f"in_{name}", v.shape, mybir.dt.from_np(v.dtype), kind="ExternalInput").ap())
    args.append(nc.dram_tensor("out_y", (B, C, HW), mybir.dt.float32, kind="ExternalOutput").ap())
    attention_conv(nc, *args)
    r = run_bass_kernel_spmd(nc, [arrays], core_ids=[0])
    return r.results[0]["out_y"].reshape(B, C, 64, 64)
```

```python
import concourse.bass as bass
from concourse import mybir
from contextlib import ExitStack

B, C, HW = 4, 256, 64 * 64
DQK = 32
CT = C // 128
CH = 512
NCH = HW // CH
MT = HW // 128
SUB = CH // 128
ALL = B * NCH
ROWS, WID = CH // 64, 64
LOWN = CH // 4
SCALE = DQK ** -0.5
EPS = 1e-5
SHIFT = 9.0
EVEN_FIRST = NCH // 2 + 1
UW = C + 1
LEAD = 2

ROUND_X, ROUND_CONV, SCAN, NEGATIVE = 9, 14, 12, 26
DOUBLE = (8, 10, 13, 15, 17, 24, 27)
TASKS = {t: [] for t in range(MT)}
TASKS[0] += [("kq",), ("u", 0)]
TASKS[2] += [("u", 1)]
TASKS[5] += [("y", 0)]
TASKS[6] += [("y", 1)]
TASKS[19] += [("low", 0)]
TASKS[20] += [("low", 1)]
TASKS[21] += [("high", 0)]
TASKS[23] += [("high", 1)]
MAXIMA = [(j, m) for j in range(SUB) for m in range(NCH)]
_left = list(MAXIMA)
for _t in range(4, 29):
    for _ in range(2 if _t in DOUBLE else 1):
        TASKS[_t].append(("max",) + _left.pop(0))
assert not _left
TASKS[29] += [("negmax",)]
NTASK = sum(len(v) for v in TASKS.values())
assert NTASK % 2 == 0
NUMBERED = {}
_n = 0
for _t in range(MT):
    NUMBERED[_t] = []
    for _task in TASKS[_t]:
        NUMBERED[_t].append((_n, _task))
        _n += 1
NUMBER = {task: n for tasks in NUMBERED.values() for n, task in tasks}
assert NUMBER[("negmax",)] == NTASK - 1
FIRST = [("wu", 0), ("wu", 1)] + [("max",) + jm for jm in MAXIMA] + [("negmax",)]
TAIL = [("y", 0), ("y", 1), ("low", 0), ("low", 1), ("high", 0), ("high", 1)]


def attention_conv(nc, x, wqk, wv, wo, phase_w, mag_w, params, gamma, alpha, out, q_dram):
    f32, f32r, f16 = mybir.dt.float32, mybir.dt.float32r, mybir.dt.float16
    ALU, ACT, AX = mybir.AluOpType, mybir.ActivationFunctionType, mybir.AxisListType
    ds = bass.ds
    x_v = x.rearrange("b (t p) (k n) -> b k p t n", p=128, n=CH)
    out_v = out.rearrange("b (t p) (k n) -> b k p t n", p=128, n=CH)

    ctx = ExitStack()
    with ctx:
        def sb(name, shape, dt=f32):
            return ctx.enter_context(nc.sbuf_tensor(name, shape, dt))

        def sem(name):
            return ctx.enter_context(nc.semaphore(name))

        kst = sb("kst", [128, 2 * HW], f32r)
        uh_flat = [sb(f"uh{i}", [128, MT * UW], f16) for i in range(2)]
        uh = [buf[:, :].rearrange("p (m n) -> p m n", n=UW) for buf in uh_flat]
        ul = [sb(f"ul{i}", [128, MT, C], f16) for i in range(2)]
        wkq = [sb(f"wkq{i}", [128, CT, 4 * DQK], f32r) for i in range(2)]
        wu = [sb(f"wu{i}", [128, CT, C], f32r) for i in range(2)]
        wp = [sb(f"wp{i}", [128, 2 * CT, C], f32r) for i in range(2)]
        wm = [sb(f"wm{i}", [128, CT, C], f32r) for i in range(2)]
        ident = sb("ident", [128, 128])
        par = sb("par", [128, 5, 2, CT])
        var = sb("var", [128, 2, CT])
        half = sb("half", [128, 2, CT])
        spare = sb("spare", [128, 3])
        quarter = sb("quarter", [128, 1])
        rstd = sb("rstd", [128, 2, CT])
        bnA = sb("bnA", [128, 2, CT])
        bnB = sb("bnB", [128, 2, CT])
        al1 = sb("al1", [128, 1])
        gam = sb("gam", [128, 1])
        losel = sb("losel", [128, 1])
        amax = sb("amax", [128, 2, NCH])
        bnd = sb("bnd", [128, 1 + CT])
        bndall = sb("bndall", [128, 1 + CT])
        bndspare = sb("bndspare", [128, 1])
        prod = sb("prod", [128, 1])
        uscale = [sb(f"uscale{i}", [128, 1]) for i in range(2)]
        ogain = sb("ogain", [128, B])
        xb, xr, xs = sb("xb", [128, CT, CH]), sb("xr", [128, CT, CH]), sb("xs", [128, CT, CH])
        xbh, xbl = sb("xbh", [128, CT, CH], f32r), sb("xbl", [128, CT, CH], f32r)
        qsave = sb("qsave", [128, CH])
        qraw = sb("qraw", [96, CH])
        qst = sb("qst", [96, CH], f32r)
        qcur = sb("qcur", [128, CH], f32r)
        pmax = sb("pmax", [128, SUB, NCH])
        nmax = sb("nmax", [128, SUB])
        nhi = sb("nhi", [128, CH], f32r)
        p32 = sb("p32", [128, 2, CH])
        ph, pl = sb("ph", [128, 4, CH], f16), sb("pl", [128, 4, CH], f16)
        oraw = sb("oraw", [128, SUB, UW])
        rs = sb("rs", [128, SUB])
        on = sb("on", [128, SUB, C])
        y = sb("y", [128, CT, ROWS, WID])
        pair = sb("pair", [128, CT, ROWS, WID // 2])
        low4 = sb("low4", [128, CT, ROWS // 2, WID // 2])
        low = sb("low", [128, CT, LOWN])
        high = sb("high", [128, CT, ROWS, WID])
        hh, hl = [sb(n, [128, CT, ROWS + 1, WID], f32r) for n in ("hh", "hl")]
        lh, ll = [sb(n, [128, CT, LOWN], f32r) for n in ("lh", "ll")]
        zlow, zlneg = sb("zlow", [128, CT, LOWN]), sb("zlneg", [128, CT, LOWN])
        z, zneg = sb("z", [128, CT, CH]), sb("zneg", [128, CT, CH])
        wraw_p = high[:, :, :, :].rearrange("p t r w -> p (t r w)").rearrange("p (t n) -> p t n", n=C)
        wraw_m = p32[:, 0, :].rearrange("p (t n) -> p t n", n=C)
        wraw_v = p32[:, 1, :].rearrange("p (t n) -> p t n", n=C)
        wraw_o = on[:, 0:CT, :]
        wraw_qk = on[:, CT:2 * CT, 0:2 * DQK]
        x0 = [buf.bitcast(f32)[:, 0:HW].rearrange("p (i t n) -> p i t n", t=CT, n=CH)
              for buf in (ul[1][:, :, :].rearrange("p m n -> p (m n)"), uh_flat[1][:, :])]
        odd_hi, odd_lo = [buf[:, :, 1:ROWS + 1, :].rearrange("p t r w -> p t (r w)") for buf in (hh, hl)]

        O = [ctx.enter_context(nc.psum_tensor(f"O{i}", [128, 512], f32)) for i in range(SUB)]
        S = [ctx.enter_context(nc.psum_tensor(f"S{i}", [128, 512], f32)) for i in range(2)]
        M = [ctx.enter_context(nc.psum_tensor(f"M{i}", [128, 512], f32)) for i in range(2)]
        PK = [[O[0], O[1], O[2]], [O[3], S[0], S[1]]]

        w_loaded, par_loaded = sem("w_loaded"), sem("par_loaded")
        x0_loaded = [sem(f"x0_loaded{c}") for c in range(NCH)]
        scan_loaded, scanned = [sem("scan_even_loaded"), sem("scan_odd_loaded")], sem("scanned")
        xb_loaded, xr_loaded, xs_loaded = sem("xb_loaded"), sem("xr_loaded"), sem("xs_loaded")
        x_hi, x_split = [sem("even_hi"), sem("odd_hi")], [sem("even_split"), sem("odd_split")]
        qsave_ready, qsave_free, qraw_loaded, qst_ready = sem("qsave_ready"), sem("qsave_free"), sem("qraw_loaded"), sem("qst_ready")
        consts, pool_step = sem("consts"), sem("pool_step")
        w_hi, w_split, wu_hi = sem("w_hi"), sem("w_split"), sem("wu_hi")
        bound, reduced, sstep, scaled, dstep = sem("bound"), sem("reduced"), sem("sstep"), sem("scaled"), sem("dstep")
        var_ready, bn_ready = sem("var_ready"), sem("bn_ready")
        proj_filled, proj_hi, proj_free = sem("proj_filled"), sem("proj_hi"), sem("proj_free")
        m_filled = [sem("m0_filled"), sem("m1_filled")]
        m_free = [sem("m0_free"), sem("m1_free")]
        q_hi, k_hi, u_hi, xs_scanned = sem("q_hi"), sem("k_hi"), sem("u_hi"), sem("xs_scanned")
        scanned0 = sem("scanned0")
        nmax_ready, nhi_ready = sem("nmax_ready"), sem("nhi_ready")
        s_filled, probs_ready, lo_ready, pv_done = sem("s_filled"), sem("probs_ready"), sem("lo_ready"), sem("pv_done")
        o01_out, o23_out, rs_step, on_ready = sem("o01_out"), sem("o23_out"), sem("rs_step"), sem("on_ready")
        pairs_ready, low_ready, high_ready = sem("pairs_ready"), sem("low_ready"), sem("high_ready")
        hh_ready, conv_in = sem("hh_ready"), sem("conv_in")
        zneg_ready = sem("zneg_ready")
        prelu_ready, out_ready, out_stored = sem("prelu_ready"), sem("out_ready"), sem("out_stored")
        low4_ready, rstd_ready, banks_set, pmax_reduced = sem("low4_ready"), sem("rstd_ready"), sem("banks_set"), sem("pmax_reduced")

        FB = (len(FIRST) + 1) // 2, len(FIRST) // 2
        UB = NTASK // 2

        def use(g, n):
            return FB[n % 2] + UB * g + n // 2

        def emptied(eng, g, task):
            n = NUMBER[task] if g is not ALL else TAIL.index(task)
            eng.wait_ge(m_free[n % 2], use(g, n) + 1)

        def turns(eng, turn, before_image=None):
            with eng.Fori(0, B // 2) as pair_i:
                for parity in range(2):
                    if before_image:
                        before_image(pair_i * 2 + parity, parity)
                    with eng.Fori(0, NCH) as c:
                        turn(pair_i * (2 * NCH) + parity * NCH + c, parity, c)

        block = ctx.enter_context(nc.Block())

        @block.sync
        def _(sp):
            sp.dma_start(wraw_v, wv.rearrange("(t p) n -> p t n", p=128)).then_inc(w_loaded, 16)
            sp.dma_start(wraw_o, wo.rearrange("(t p) n -> p t n", p=128)).then_inc(w_loaded, 16)
            sp.dma_start(wraw_qk, wqk.rearrange("(t p) n -> p t n", p=128)).then_inc(w_loaded, 16)
            for c in range(2):
                sp.dma_start(x0[c % 2][:, c // 2], x_v[0, c]).then_inc(x0_loaded[c], 16)
            sp.dma_start(wraw_p, phase_w.rearrange("(t p) n -> p t n", p=128)).then_inc(w_loaded, 16)
            sp.dma_start(wraw_m, mag_w.rearrange("(t p) n -> p t n", p=128)).then_inc(w_loaded, 16)
            sp.dma_start(par[:, :, :, :], params).then_inc(par_loaded, 16)
            sp.dma_start(gam[:, :], gamma.partition_broadcast(128)).then_inc(par_loaded, 16)
            sp.dma_start(al1[:, :], alpha.partition_broadcast(128)).then_inc(par_loaded, 16)
            for c in range(2, NCH):
                sp.dma_start(x0[c % 2][:, c // 2], x_v[0, c]).then_inc(x0_loaded[c], 16)
            sp.dma_start(xb[:, :, :], x_v[1, 0]).then_inc(xb_loaded, 16)

            def fetch_q(slot):
                for s in range(3):
                    src = q_dram[slot] if isinstance(slot, int) else q_dram[slot].rearrange("k q n -> (k q) n")
                    sp.dma_start(qraw[s * DQK:(s + 1) * DQK, :], src).then_inc(qraw_loaded, 16)

            for c in range(2):
                sp.dma_start((xr, xs)[c % 2][:, :, :], x_v[1, c]).then_inc(scan_loaded[c % 2], 16)
            for c in range(NCH):
                sp.wait_ge(qsave_ready, c + 1)
                sp.dma_start(q_dram[c], qsave[96:128, :]).then_inc(qsave_free, 16)
                if c + 2 < NCH:
                    sp.wait_ge(scanned, c + 1)
                    sp.dma_start((xr, xs)[c % 2][:, :, :], x_v[1, c + 2]).then_inc(scan_loaded[c % 2], 16)
            sp.wait_ge(qsave_free, 16 * (NCH + 1))
            fetch_q(0)
            sp.wait_ge(qst_ready, 1)
            fetch_q(1)
            sp.wait_ge(scanned, NCH)
            sp.dma_start(xr[:, :, :], x_v[B - 1, NCH - 1]).then_inc(xr_loaded, 16)
            sp.dma_start(xs[:, :, :], x_v[2, 0]).then_inc(xs_loaded, 16)

            def turn(g, parity, c):
                sp.wait_ge(qsave_ready, NCH + g + 1)
                sp.dma_start(q_dram[ds(c, 1)].rearrange("k q n -> (k q) n"), qsave[96:128, :]).then_inc(qsave_free, 16)
                sp.wait_ge(qst_ready, g + 2)
                sp.wait_ge(qsave_free, 16 * (NCH + g + 2))
                fetch_q(ds((c + 2) % NCH, 1))
                sp.wait_ge(x_split[0], EVEN_FIRST + g)
                gk = (g + 1 + NCH) % ALL
                sp.dma_start(xb[:, :, :], x_v[ds(gk // NCH, 1), ds(gk % NCH, 1)]).then_inc(xb_loaded, 16)
                emptied(sp, g, ("y", 1))
                sp.dma_start(xr[:, :, :], x_v[ds(g // NCH, 1), ds(g % NCH, 1)]).then_inc(xr_loaded, 16)
                sp.wait_ge(xs_scanned, g + 2)
                gs = (g + 1 + 2 * NCH) % ALL
                sp.dma_start(xs[:, :, :], x_v[ds(gs // NCH, 1), ds(gs % NCH, 1)]).then_inc(xs_loaded, 16)
                sp.wait_ge(out_ready, g + 2)
                gp = (g + (ALL - 1)) % ALL
                sp.dma_start(out_v[ds(gp // NCH, 1), ds(gp % NCH, 1)], z[:, :, :]).then_inc(out_stored, 16)

            turns(sp, turn)
            sp.wait_ge(out_ready, ALL + 2)
            sp.dma_start(out_v[B - 1, NCH - 1], z[:, :, :]).then_inc(out_stored, 16)
            sp.wait_ge(out_stored, 16 * (ALL + 2))
            sp.wait_ge(xb_loaded, 16 * (1 + ALL))
            sp.wait_ge(xs_loaded, 16 * (1 + ALL))
            sp.wait_ge(xr_loaded, 16 * (1 + ALL))
            sp.wait_ge(qraw_loaded, 16 * 3 * (2 + ALL))
            sp.wait_ge(qsave_free, 16 * (1 + NCH + ALL))

        @block.tensor
        def _(pe):
            def wide(bank, stat, mov, last=None):
                products = [(a, b) for pa, pb in ((0, 0), (0, 1), (1, 0)) for a, b in zip(stat[pa], mov[pb])]
                for i, (a, b) in enumerate(products):
                    ins = nc.tensor.matmul(bank, a, b, start=(i == 0), stop=(i == len(products) - 1))
                return ins

            def project_kq(bank, xs):
                return wide(bank[:, :], [[wkq[v][:, t, :] for t in range(CT)] for v in range(2)],
                            [[xs[v][:, t, :] for t in range(CT)] for v in range(2)])

            def project_u(bank, xs, half_i):
                for m in range(2):
                    px = slice((2 * half_i + m) * 128, (2 * half_i + m + 1) * 128)
                    ins = wide(bank[:, m * C:(m + 1) * C], [[xs[v][:, t, px] for t in range(CT)] for v in range(2)],
                               [[wu[v][:, t, :] for t in range(CT)] for v in range(2)])
                return ins

            def transposed(bank, h):
                for j in range(SUB):
                    ins = nc.tensor.transpose(bank[:, j * 128:(j + 1) * 128], on[:, j, h * 128:(h + 1) * 128], ident[:, :])
                return ins

            def low_conv(bank, o):
                return wide(bank[:, 0:LOWN], [[wm[v][:, t, o * 128:(o + 1) * 128] for t in range(CT)] for v in range(2)],
                            [[(lh, ll)[v][:, t, :] for t in range(CT)] for v in range(2)])

            def high_conv(bank, oh):
                return wide(bank[:, :], [[wp[v][:, s * CT + t, oh * 128:(oh + 1) * 128] for s in range(2) for t in range(CT)]
                                         for v in range(2)],
                            [[(hh, hl)[v][:, t, 1 - s:1 - s + ROWS, :].rearrange("p r w -> p (r w)")
                              for s in range(2) for t in range(CT)] for v in range(2)])

            def max_scores(bank, j, keys_at):
                return nc.tensor.matmul(bank[:, :], qst[:, j * 128:(j + 1) * 128], kst[0:96, keys_at],
                                        start=True, stop=True)

            def negmax_rows(bank):
                for j in range(SUB):
                    ins = nc.tensor.transpose(bank[:, j * 128:(j + 1) * 128],
                                              nmax[:, j:j + 1].to_broadcast([128, 128]), ident[:, :])
                return ins

            pe.wait_ge(w_loaded, 5 * 16)
            pe.wait_ge(consts, 1)
            for n in range(2):
                for t in range(CT):
                    ins = nc.tensor.matmul(M[n][:, 0:C], wraw_v[:, t, n * 128:(n + 1) * 128],
                                           wraw_o[:, t, :], start=(t == 0), stop=(t == CT - 1))
                ins.then_inc(m_filled[n], 1)
            nc.tensor.transpose(O[0][:, 0:128], ident[:, :], ident[:, :]).then_inc(pv_done, 1)
            pe.wait_ge(w_split, 1)
            for n in range(CT):
                pe.wait_ge(m_free[n], 1)
            with pe.Fori(0, NCH // 2) as i:
                for s, xs in ((0, (xbh, xbl)), (1, (odd_hi, odd_lo))):
                    pe.wait_ge(x_split[s], i + 1)
                    pe.wait_ge(proj_free, 6 * i + 3 * s + 1)
                    project_kq(PK[s][0], xs).then_inc(proj_filled, 1)
                    for hf in range(2):
                        project_u(PK[s][1 + hf], xs, hf).then_inc(proj_filled, 1)
            pe.wait_ge(qst_ready, 1)
            pe.wait_ge(proj_free, 4 + 3 * NCH)
            for n in range(2, len(FIRST)):
                pe.wait_ge(m_free[n % 2], n // 2)
                if FIRST[n][0] == "max":
                    _, j, m = FIRST[n]
                    max_scores(M[n % 2], j, slice(m * CH, (m + 1) * CH)).then_inc(m_filled[n % 2], 1)
                else:
                    pe.wait_ge(nmax_ready, 1)
                    negmax_rows(M[n % 2]).then_inc(m_filled[n % 2], 1)
            pe.wait_ge(m_free[0], FB[0])

            def scores(g, parity, t):
                if t >= LEAD:
                    pe.wait_ge(probs_ready, MT * g + t - 1)
                at = parity * HW + t * 128
                nc.tensor.matmul(S[t % 2][:, :], kst[:, at:at + 128], qcur[:, :],
                                 start=True, stop=True).then_inc(s_filled, 1)

            def tasks(g, keys_next, t):
                for n, task in NUMBERED[t]:
                    kind = task[0]
                    bank = M[n % 2]
                    pe.wait_ge(m_free[n % 2], use(g, n))
                    if kind in ("kq", "u"):
                        pe.wait_ge(x_split[0], EVEN_FIRST + g)
                        ins = project_kq(bank, (xbh, xbl)) if kind == "kq" else project_u(bank, (xbh, xbl), task[1])
                    elif kind == "y":
                        pe.wait_ge(on_ready, g + 2)
                        ins = transposed(bank, task[1])
                    elif kind == "low":
                        pe.wait_ge(conv_in, g + 1)
                        ins = low_conv(bank, task[1])
                    elif kind == "high":
                        ins = high_conv(bank, task[1])
                    elif kind == "max":
                        _, j, m = task
                        if (j, m) == MAXIMA[0]:
                            pe.wait_ge(qst_ready, g + 2)
                            emptied(pe, g, ("kq",))
                        ins = max_scores(bank, j, ds(keys_next + m * CH, CH))
                    else:
                        pe.wait_ge(nmax_ready, g + 2)
                        ins = negmax_rows(bank)
                    ins.then_inc(m_filled[n % 2], 1)

            def weigh(g, parity, t):
                pe.wait_ge(lo_ready, MT * g + t + 1)
                for j in range(SUB):
                    if t == 0:
                        pe.wait_ge((o01_out, o23_out)[j // 2], 2 * g + j % 2 + 1)
                    q = slice(j * 128, (j + 1) * 128)
                    nc.tensor.matmul(O[j][:, 0:UW], ph[:, t % 4, q], uh[parity][:, t, :], start=(t == 0), stop=False)
                    nc.tensor.matmul(O[j][:, 0:C], ph[:, t % 4, q], ul[parity][:, t, :], start=False, stop=False)
                    ins = nc.tensor.matmul(O[j][:, 0:UW], pl[:, t % 4, q], uh[parity][:, t, :],
                                           start=False, stop=(t == MT - 1))
                ins.then_inc(pv_done, 1)

            def turn(g, parity, c):
                keys_next = pe.snap(((c + (parity * NCH + 1)) // NCH) % 2 * HW)
                pe.wait_ge(m_free[1], use(g, 1))
                for t in range(LEAD):
                    scores(g, parity, t)
                for t in range(MT):
                    if t == 0:
                        tasks(g, keys_next, t)
                    if t + LEAD < MT:
                        scores(g, parity, t + LEAD)
                    if t > 0:
                        tasks(g, keys_next, t)
                    weigh(g, parity, t)

            turns(pe, turn)
            for n, task in enumerate(TAIL):
                pe.wait_ge(m_free[n % 2], use(ALL, n))
                if task[0] == "y":
                    pe.wait_ge(on_ready, ALL + 2)
                    ins = transposed(M[n % 2], task[1])
                elif task[0] == "low":
                    pe.wait_ge(conv_in, ALL + 1)
                    ins = low_conv(M[n % 2], task[1])
                else:
                    ins = high_conv(M[n % 2], task[1])
                ins.then_inc(m_filled[n % 2], 1)

        @block.scalar
        def _(act):
            act.wait_ge(w_loaded, 5 * 16)
            for s in range(4):
                src = slice(DQK, 2 * DQK) if s < 3 else slice(0, DQK)
                nc.scalar.activation(wkq[0][:, :, s * DQK:(s + 1) * DQK], wraw_qk[:, :, src], ACT.Copy)
            nc.scalar.activation(wp[0][:, :, :], wraw_p, ACT.Copy)
            nc.scalar.activation(wm[0][:, :, :], wraw_m, ACT.Copy).then_inc(w_hi, 1)
            for n in range(CT):
                act.wait_ge(m_filled[n], 1)
                nc.scalar.activation(wu[0][:, n, :], M[n][:, 0:C], ACT.Copy).then_inc(wu_hi, 1)
            for s, hi in ((0, xbh[:, :, :]), (1, odd_hi)):
                act.wait_ge(x0_loaded[s], 16)
                nc.scalar.activation(hi, x0[s][:, 0], ACT.Copy).then_inc(x_hi[s], 1)
            act.wait_ge(scaled, 1)
            for c in range(2, NCH):
                act.wait_ge(x0_loaded[c], 16)

            def take_projections(i, s):
                filled = 6 * i + 3 * s
                act.wait_ge(proj_filled, filled + 1)
                nc.scalar.activation(kst[0:96, ds((2 * i + s) * CH, CH)], PK[s][0][0:96, :], ACT.Copy).then_inc(proj_hi, 1)
                act.wait_ge(qsave_free, 16 * (2 * i + s + 1))
                nc.scalar.activation(qsave[96:128, :], PK[s][0][96:128, :], ACT.Copy).then_inc(qsave_ready, 1)
                for hf in range(2):
                    act.wait_ge(proj_filled, filled + 2 + hf)
                    nc.scalar.activation(uh[0][:, ds((2 * i + s) * SUB + 2 * hf, 2), 0:C],
                                         PK[s][1 + hf][:, :].rearrange("p (m n) -> p m n", n=C),
                                         ACT.Copy, scale=uscale[0][:, 0:1]).then_inc(proj_hi, 1)

            with act.Fori(0, NCH // 2 - 1) as i:
                for s, hi in ((0, xbh[:, :, :]), (1, odd_hi)):
                    take_projections(i, s)
                    nc.scalar.activation(hi, x0[s][:, ds(i + 1, 1)].rearrange("p i t n -> p (i t) n"), ACT.Copy).then_inc(x_hi[s], 1)
            take_projections(NCH // 2 - 1, 0)
            act.wait_ge(xb_loaded, 16)
            nc.scalar.activation(xbh[:, :, :], xb[:, :, :], ACT.Copy).then_inc(x_hi[0], 1)
            take_projections(NCH // 2 - 1, 1)
            act.wait_ge(qraw_loaded, 16 * 3)
            nc.scalar.activation(qst[:, :], qraw[:, :], ACT.Copy).then_inc(q_hi, 1)
            act.wait_ge(bn_ready, 1)
            act.wait_ge(banks_set, 1)

            def copy_out(g, j):
                act.wait_ge(pv_done, MT * g + 1)
                act.wait_ge(on_ready, g + 1)
                nc.scalar.activation(oraw[:, j, :], O[j][:, 0:UW], ACT.Copy).then_inc(o01_out, 1)

            def probabilities(g, t):
                act.wait_ge(s_filled, MT * g + t + 1)
                if t >= 4:
                    act.wait_ge(pv_done, MT * g + t - 2)
                nc.scalar.activation(ph[:, t % 4, :], S[t % 2][:, :], ACT.Exp, scale=SCALE)
                if t >= 2:
                    act.wait_ge(lo_ready, MT * g + t - 1)
                nc.scalar.activation(p32[:, t % 2, :], S[t % 2][:, :], ACT.Exp, scale=SCALE).then_inc(probs_ready, 1)

            def take(bank, task, g, parity, c):
                kind = task[0]
                if kind == "kq":
                    nc.scalar.activation(kst[0:96, ds(c * CH + (1 - parity) * HW, CH)], bank[0:96, :], ACT.Copy).then_inc(k_hi, 1)
                    act.wait_ge(qsave_free, 16 * (NCH + g + 1))
                    nc.scalar.activation(qsave[96:128, :], bank[96:128, :], ACT.Copy).then_inc(qsave_ready, 1)
                elif kind == "u":
                    nc.scalar.activation(uh[1 - parity][:, ds(c * SUB + 2 * task[1], 2), 0:C],
                                         bank[:, :].rearrange("p (m n) -> p m n", n=C),
                                         ACT.Copy, scale=uscale[1 - parity][:, 0:1]).then_inc(u_hi, 1)

            def norm_low(bank, g, o, free):
                act.wait_ge(out_ready, g + 1)
                nc.scalar.activation(zlow[:, o, :], bank[:, 0:LOWN], ACT.Identity, scale=bnA[:, 0, o:o + 1],
                                     bias=bnB[:, 0, o:o + 1]).then_inc(free, 1)

            def norm_high(bank, g, o, free):
                act.wait_ge(out_stored, 16 * g + 16)
                nc.scalar.activation(z[:, o, :], bank[:, :], ACT.Identity, scale=bnA[:, 1, o:o + 1],
                                     bias=bnB[:, 1, o:o + 1]).then_inc(free, 1)

            def round_conv(g):
                act.wait_ge(high_ready, g + 2)
                nc.scalar.activation(hh[:, :, 1:ROWS + 1, :], high[:, :, :, :], ACT.Copy)
                nc.scalar.activation(hh[:, :, 0, :], high[:, :, ROWS - 1, :], ACT.Copy)
                nc.scalar.activation(lh[:, :, :], low[:, :, :], ACT.Copy).then_inc(hh_ready, 1)

            def turn(g, parity, c):
                copy_out(g, 0)
                probabilities(g, 0)
                copy_out(g, 1)
                probabilities(g, 1)
                for t in range(MT):
                    if 0 < t < MT - LEAD:
                        probabilities(g, t + LEAD)
                    for n, task in NUMBERED[t]:
                        bank = M[n % 2]
                        if task[0] in ("kq", "u", "low", "high"):
                            act.wait_ge(m_filled[n % 2], use(g, n) + 1)
                        if task[0] == "low":
                            norm_low(bank, g, task[1], m_free[n % 2])
                        elif task[0] == "high":
                            norm_high(bank, g, task[1], m_free[n % 2])
                        else:
                            take(bank, task, g, parity, c)
                    if t == 0:
                        probabilities(g, LEAD)
                        act.wait_ge(m_free[1], use(g, 1))
                        act.wait_ge(qraw_loaded, 16 * 3 * (g + 2))
                        nc.scalar.activation(qst[:, :], qraw[:, :], ACT.Copy).then_inc(q_hi, 1)
                    if t == ROUND_X:
                        act.wait_ge(xb_loaded, (g + 2) * 16)
                        nc.scalar.activation(xbh[:, :, :], xb[:, :, :], ACT.Copy).then_inc(x_hi[0], 1)
                    if t == ROUND_CONV:
                        round_conv(g)

            def before_image(image, parity):
                act.wait_ge(scaled, image + 2)

            turns(act, turn, before_image)
            copy_out(ALL, 0)
            copy_out(ALL, 1)
            round_conv(ALL)
            for n, task in enumerate(TAIL):
                if task[0] != "y":
                    act.wait_ge(m_filled[n % 2], use(ALL, n) + 1)
                    if task[0] == "low":
                        norm_low(M[n % 2], ALL, task[1], m_free[n % 2])
                    else:
                        norm_high(M[n % 2], ALL, task[1], m_free[n % 2])

        @block.vector
        def _(dve):
            chain = [0]

            def done(ins):
                chain[0] += 1
                ins.then_inc(dstep, 1)
                dve.wait_ge(dstep, chain[0])

            nc.vector.memset(half[:, :, :], -0.5).then_inc(on_ready, 1)
            nc.vector.memset(quarter[:, :], 0.25).then_inc(out_stored, 16)
            nc.vector.memset(uh[0][:, :, C:C + 1], 1.0).then_inc(qsave_free, 16)
            nc.vector.memset(ogain[:, :], 1.0).then_inc(xs_scanned, 1)
            dve.wait_ge(par_loaded, 3 * 16)
            done(nc.vector.tensor_scalar(var[:, :, :], par[:, 4, :, :], EPS, None, ALU.add))
            nc.vector.tensor_scalar(al1[:, :], al1[:, :], 1.0, None, ALU.subtract).then_inc(var_ready, 1)
            dve.wait_ge(consts, 1)
            done(nc.vector.tensor_tensor(prod[:, :], ident[:, 96:97], ident[:, 97:98], ALU.add))
            nc.vector.tensor_scalar(kst[96:128, :], ident[96:128, 0:1].to_broadcast([32, 2 * HW]), 0.0,
                                    prod[96:128, 0:1], ALU.mult, ALU.add)
            done(nc.vector.tensor_scalar(losel[:, :], ident[:, 96:97], 1.0, None, ALU.subtract))
            dve.wait_ge(rstd_ready, 1)
            done(nc.vector.tensor_tensor(bnA[:, :, :], par[:, 1, :, :], rstd[:, :, :], ALU.mult))
            done(nc.vector.tensor_tensor(bnB[:, :, :], par[:, 0, :, :], par[:, 3, :, :], ALU.subtract))
            done(nc.vector.tensor_tensor(bnB[:, :, :], bnB[:, :, :], bnA[:, :, :], ALU.mult))
            nc.vector.tensor_tensor(bnB[:, :, :], bnB[:, :, :], par[:, 2, :, :], ALU.add).then_inc(bn_ready, 1)
            dve.wait_ge(w_hi, 1)
            for s in range(4):
                src = slice(DQK, 2 * DQK) if s < 3 else slice(0, DQK)
                cols = slice(s * DQK, (s + 1) * DQK)
                nc.vector.tensor_tensor(wkq[1][:, :, cols], wraw_qk[:, :, src], wkq[0][:, :, cols].bitcast(f32), ALU.subtract)
            nc.vector.tensor_tensor(wp[1][:, :, :], wraw_p, wp[0][:, :, :].bitcast(f32), ALU.subtract)
            nc.vector.tensor_tensor(wm[1][:, :, :], wraw_m, wm[0][:, :, :].bitcast(f32), ALU.subtract).then_inc(w_split, 1)
            for n in range(CT):
                dve.wait_ge(wu_hi, n + 1)
                nc.vector.tensor_reduce(bnd[:, 1 + n:2 + n], M[n][:, 0:C], AX.X, ALU.max, apply_absolute_value=True)
                nc.vector.tensor_tensor(wu[1][:, n, :], M[n][:, 0:C], wu[0][:, n, :].bitcast(f32),
                                        ALU.subtract).then_inc(m_free[n], 1)

            def scan(at, xs, counted):
                nc.vector.tensor_reduce(at, xs.rearrange("p t n -> p (t n)"), AX.X, ALU.max,
                                        apply_absolute_value=True).then_inc(counted, 1)

            def find_scale(image, parity):
                nc.vector.tensor_reduce(bnd[:, 0:1], amax[:, parity, :], AX.X, ALU.max).then_inc(bound, 1)
                dve.wait_ge(reduced, image + 1)
                nc.vector.tensor_tensor(prod[:, :], bndall[:, 1:2], bndall[:, 2:3], ALU.max).then_inc(sstep, 1)
                dve.wait_ge(sstep, 3 * image + 1)
                nc.vector.tensor_tensor(prod[:, :], prod[:, :], bndall[:, 0:1], ALU.mult).then_inc(sstep, 1)
                dve.wait_ge(sstep, 3 * image + 2)
                nc.vector.tensor_scalar(prod[:, :], prod[:, :], C / 2.0 ** 15, 1e-30, ALU.mult, ALU.max).then_inc(sstep, 1)
                dve.wait_ge(sstep, 3 * image + 3)
                gain = ogain[:, 0:1] if isinstance(image, int) else ogain[:, ds(image % B, 1)]
                nc.vector.tensor_tensor(gain, prod[:, :], gam[:, :], ALU.mult)
                nc.vector.reciprocal(uscale[parity][:, :], prod[:, :]).then_inc(scaled, 1)

            def split_x(s, lo, xs, hi, count):
                dve.wait_ge(x_hi[s], count)
                nc.vector.tensor_tensor(lo, xs, hi.bitcast(f32), ALU.subtract).then_inc(x_split[s], 1)

            for c in range(NCH):
                dve.wait_ge(x0_loaded[c], 16)
                scan(amax[:, 0, c:c + 1], x0[c % 2][:, c // 2], scanned0)
                if c == 1:
                    split_x(0, xbl[:, :, :], x0[0][:, 0], xbh[:, :, :], 1)
                    split_x(1, odd_lo, x0[1][:, 0], odd_hi, 1)
            dve.wait_ge(scanned0, NCH)
            find_scale(0, 0)

            def take_projections(i, s):
                filled = 6 * i + 3 * s
                dve.wait_ge(proj_hi, filled + 1)
                keys = kst[32:64, ds((2 * i + s) * CH, CH)]
                nc.vector.tensor_tensor(keys, PK[s][0][32:64, :], keys.bitcast(f32), ALU.subtract).then_inc(proj_free, 1)
                for hf in range(2):
                    dve.wait_ge(proj_hi, filled + 2 + hf)
                    tiles = ds((2 * i + s) * SUB + 2 * hf, 2)
                    nc.vector.scalar_tensor_tensor(ul[0][:, tiles, :], PK[s][1 + hf][:, :].rearrange("p (m n) -> p m n", n=C),
                                                   uscale[0][:, 0:1], uh[0][:, tiles, 0:C], ALU.mult, ALU.subtract)\
                        .then_inc(proj_free, 1)

            def scan_next(i, s):
                dve.wait_ge(scan_loaded[s], (i + 1) * 16)
                scan(amax[:, 1, ds(2 * i + s, 1)], (xr, xs)[s][:, :, :], scanned)

            nc.vector.memset(spare[:, 2:3], 0.0).then_inc(proj_free, 4)
            with dve.Fori(0, NCH // 2 - 1) as i:
                for s, lo, hi in ((0, xbl[:, :, :], xbh[:, :, :]), (1, odd_lo, odd_hi)):
                    take_projections(i, s)
                    split_x(s, lo, x0[s][:, ds(i + 1, 1)].rearrange("p i t n -> p (i t) n"), hi, i + 2)
                    scan_next(i, s)
            take_projections(NCH // 2 - 1, 0)
            split_x(0, xbl[:, :, :], xb[:, :, :], xbh[:, :, :], EVEN_FIRST)
            take_projections(NCH // 2 - 1, 1)
            dve.wait_ge(proj_free, 4 + 3 * NCH)
            nc.vector.memset(uh[1][:, :, C:C + 1], 1.0)
            for j in range(SUB):
                ins = nc.vector.memset(O[j][:, :], 1.0)
            ins.then_inc(banks_set, 1)

            def low_q(count):
                dve.wait_ge(q_hi, count)
                nc.vector.tensor_tensor(qst[64:96, :], qraw[64:96, :], qst[64:96, :].bitcast(f32),
                                        ALU.subtract).then_inc(qst_ready, 1)

            def partial_max(bank, j, m, free):
                nc.vector.tensor_reduce(pmax[:, j, m:m + 1], bank[:, :], AX.X, ALU.max).then_inc(free, 1)

            def maxima(count):
                nc.vector.tensor_reduce(nmax[:, :], pmax[:, :, :], AX.X, ALU.max, negate=True).then_inc(pmax_reduced, 1)
                dve.wait_ge(pmax_reduced, count)
                nc.vector.tensor_scalar(nmax[:, :], nmax[:, :], SHIFT / SCALE, None, ALU.add).then_inc(nmax_ready, 1)

            def finish_q(bank, count, free):
                dve.wait_ge(nhi_ready, count)
                nc.vector.tensor_copy(qcur[0:96, :], qst[:, :].bitcast(f32))
                nc.vector.scalar_tensor_tensor(qcur[96:128, :], nhi[96:128, :].bitcast(f32), losel[96:128, 0:1],
                                               bank[96:128, :], ALU.mult, ALU.add).then_inc(free, 1)

            low_q(1)
            for n in range(2, len(FIRST)):
                kind, bank, free = FIRST[n][0], M[n % 2], m_free[n % 2]
                dve.wait_ge(m_filled[n % 2], n // 2 + 1)
                if kind == "max":
                    partial_max(bank, *FIRST[n][1:], free)
                    if FIRST[n][1:] == MAXIMA[-1]:
                        dve.wait_ge(free, n // 2 + 1)
                        maxima(1)
                else:
                    nc.vector.tensor_copy(nhi[96:128, :], bank[96:128, :]).then_inc(nhi_ready, 1)
                    finish_q(bank, 1, free)
            for s in range(2):
                scan_next(NCH // 2 - 1, s)
            dve.wait_ge(scanned, NCH)

            def copy_out(g, j):
                dve.wait_ge(pv_done, MT * g + 1)
                dve.wait_ge(on_ready, g + 1)
                nc.vector.tensor_copy(oraw[:, j, :], O[j][:, 0:UW]).then_inc(o23_out, 1)

            def normalise(g):
                dve.wait_ge(o01_out, 2 * g + 2)
                dve.wait_ge(o23_out, 2 * g + 2)
                nc.vector.reciprocal(rs[:, :], oraw[:, :, C]).then_inc(rs_step, 1)
                dve.wait_ge(rs_step, 2 * g + 1)
                gain = ogain[:, B - 1:B] if isinstance(g, int) else ogain[:, ds((g + (ALL - 1)) % ALL // NCH, 1)]
                nc.vector.tensor_tensor(rs[:, :], rs[:, :], gain.to_broadcast([128, SUB]), ALU.mult).then_inc(rs_step, 1)
                dve.wait_ge(rs_step, 2 * g + 2)
                for j in range(SUB):
                    ins = nc.vector.tensor_scalar(on[:, j, :], oraw[:, j, 0:C], rs[:, j:j + 1], None, ALU.mult)
                ins.then_inc(on_ready, 1)

            def low_probabilities(g, t):
                dve.wait_ge(probs_ready, MT * g + t + 1)
                nc.vector.tensor_tensor(pl[:, t % 4, :], p32[:, t % 2, :], ph[:, t % 4, :], ALU.subtract).then_inc(lo_ready, 1)

            def add_residual(bank, g, h, free):
                if h == 0:
                    dve.wait_ge(xr_loaded, 16 * g + 16)
                    dve.wait_ge(high_ready, g + 1)
                nc.vector.tensor_tensor(y[:, h, :, :].rearrange("p r w -> p (r w)"), bank[:, :], xr[:, h, :],
                                        ALU.add).then_inc(free, 1)

            def negative_parts(g):
                emptied(dve, g, ("low", 0))
                emptied(dve, g, ("low", 1))
                nc.vector.tensor_scalar(zlneg[:, :, :], zlow[:, :, :], 0.0, al1[:, 0:1], ALU.min, ALU.mult)
                emptied(dve, g, ("high", 0))
                emptied(dve, g, ("high", 1))
                nc.vector.tensor_scalar(zneg[:, :, :], z[:, :, :], 0.0, al1[:, 0:1], ALU.min, ALU.mult).then_inc(zneg_ready, 1)

            def take(n, task, g, parity, c):
                kind, bank, free = task[0], M[n % 2], m_free[n % 2]
                if kind == "kq":
                    dve.wait_ge(k_hi, g + 1)
                    dve.wait_ge(qsave_ready, NCH + g + 1)
                    keys = kst[32:64, ds(c * CH + (1 - parity) * HW, CH)]
                    nc.vector.tensor_tensor(keys, bank[32:64, :], keys.bitcast(f32), ALU.subtract).then_inc(free, 1)
                elif kind == "u":
                    dve.wait_ge(u_hi, 2 * g + 1 + task[1])
                    tiles = ds(c * SUB + 2 * task[1], 2)
                    nc.vector.scalar_tensor_tensor(ul[1 - parity][:, tiles, :], bank[:, :].rearrange("p (m n) -> p m n", n=C),
                                                   uscale[1 - parity][:, 0:1], uh[1 - parity][:, tiles, 0:C], ALU.mult, ALU.subtract)\
                        .then_inc(free, 1)
                elif kind in ("y", "max", "negmax"):
                    dve.wait_ge(m_filled[n % 2], use(g, n) + 1)
                    if kind == "y":
                        add_residual(bank, g, task[1], free)
                    elif kind == "max":
                        partial_max(bank, task[1], task[2], free)
                        if task[1:] == MAXIMA[-1]:
                            emptied(dve, g, task)
                            maxima(g + 2)
                    else:
                        nc.vector.tensor_copy(nhi[96:128, :], bank[96:128, :]).then_inc(nhi_ready, 1)

            def turn(g, parity, c):
                copy_out(g, 2)
                copy_out(g, 3)
                low_probabilities(g, 0)
                for t in range(MT):
                    if t + 1 < MT:
                        low_probabilities(g, t + 1)
                    if t == 0:
                        normalise(g)
                    if t == 1:
                        low_q(g + 2)
                    if t == SCAN:
                        dve.wait_ge(xs_loaded, (g + 1) * 16)
                        scan(amax[:, parity, ds(c, 1)], xs[:, :, :], xs_scanned)
                    for n, task in NUMBERED[t]:
                        take(n, task, g, parity, c)
                    if t == NEGATIVE:
                        negative_parts(g)
                dve.wait_ge(s_filled, MT * g + MT)
                finish_q(M[(NTASK - 1) % 2], g + 2, m_free[(NTASK - 1) % 2])

            def before_image(image, parity):
                dve.wait_ge(xs_scanned, image * NCH + 1)
                find_scale(image + 1, 1 - parity)

            turns(dve, turn, before_image)
            copy_out(ALL, 2)
            copy_out(ALL, 3)
            normalise(ALL)
            for n, task in enumerate(TAIL[:CT]):
                dve.wait_ge(m_filled[n % 2], use(ALL, n) + 1)
                add_residual(M[n % 2], ALL, task[1], m_free[n % 2])
            negative_parts(ALL)

        @block.gpsimd
        def _(pool):
            nc.gpsimd.memset(ident[:, :], 0.0).then_inc(pool_step, 1)
            pool.wait_ge(pool_step, 1)
            nc.gpsimd.affine_select(out=ident[:, :], in_=ident[:, :], compare_op=ALU.not_equal, fill=1.0, base=0,
                                    pattern=[[-1, 128]], channel_multiplier=1).then_inc(consts, 1)
            nc.gpsimd.memset(spare[:, 0:1], 0.0).then_inc(out_ready, 1)
            nc.gpsimd.memset(spare[:, 1:2], 0.0).then_inc(high_ready, 1)
            pool.wait_ge(var_ready, 1)
            nc.gpsimd.tensor_tensor(rstd[:, :, :], var[:, :, :], half[:, :, :], ALU.pow).then_inc(rstd_ready, 1)

            def reduce_bound(image):
                pool.wait_ge(bound, image + 1)
                nc.gpsimd.tensor_tensor(bndspare[:, :], bnd[:, 0:1], bnd[:, 0:1], ALU.add)
                nc.gpsimd.partition_all_reduce(bndall[:, :], bnd[:, :], 128, bass.bass_isa.ReduceOp.max).then_inc(reduced, 1)

            reduce_bound(0)

            HR = ROWS // 2

            def rows(buf, t, r):
                return buf[:, t, :, :].rearrange("p (h two) (w s) -> p two h w s", two=2, s=2)[:, r]

            def spread(buf, t):
                return buf[:, t, :].rearrange("p (h w a) -> p h w a", h=HR, a=1).to_broadcast([128, HR, WID // 2, 2])

            def split_frequencies(g):
                emptied(pool, g, ("y", 1))
                for t in range(CT):
                    yp = y[:, t, :, :].rearrange("p r (w s) -> p s r w", s=2)
                    ins = nc.gpsimd.tensor_tensor(pair[:, t, :, :], yp[:, 0], yp[:, 1], ALU.add)
                ins.then_inc(pairs_ready, 1)
                pool.wait_ge(pairs_ready, g + 1)
                pp = pair[:, :, :, :].rearrange("p t (h s) w -> p s (t h) w", s=2)
                nc.gpsimd.tensor_tensor(low4[:, :, :, :].rearrange("p t h w -> p (t h) w"), pp[:, 0], pp[:, 1],
                                        ALU.add).then_inc(low4_ready, 1)
                pool.wait_ge(low4_ready, g + 1)
                nc.gpsimd.tensor_tensor(low[:, :, :].rearrange("p t n -> p (t n)"),
                                        low4[:, :, :, :].rearrange("p t h w -> p (t h w)"),
                                        quarter[:, 0:1].to_broadcast([128, CT * LOWN]), ALU.mult).then_inc(low_ready, 1)
                pool.wait_ge(low_ready, g + 1)
                for t in range(CT):
                    for r in range(2):
                        ins = nc.gpsimd.tensor_tensor(rows(high, t, r), rows(y, t, r), spread(low, t), ALU.subtract)
                ins.then_inc(high_ready, 1)

            def low_x(g):
                pool.wait_ge(x_hi[0], g + EVEN_FIRST + 1)
                for t in range(CT):
                    for px in (slice(0, CH // 2), slice(CH // 2, CH)):
                        ins = nc.gpsimd.tensor_tensor(xbl[:, t, px], xb[:, t, px], xbh[:, t, px].bitcast(f32), ALU.subtract)
                ins.then_inc(x_split[0], 1)

            def low_conv_in(g):
                pool.wait_ge(hh_ready, g + 1)
                for t in range(CT):
                    for r in (0, HR):
                        nc.gpsimd.tensor_tensor(hl[:, t, 1 + r:1 + r + HR, :], high[:, t, r:r + HR, :],
                                                hh[:, t, 1 + r:1 + r + HR, :].bitcast(f32), ALU.subtract)
                nc.gpsimd.tensor_tensor(hl[:, :, 0, :], high[:, :, ROWS - 1, :], hh[:, :, 0, :].bitcast(f32), ALU.subtract)
                nc.gpsimd.tensor_tensor(ll[:, :, :], low[:, :, :], lh[:, :, :].bitcast(f32), ALU.subtract).then_inc(conv_in, 1)

            def add_up(g):
                pool.wait_ge(zneg_ready, g + 1)
                nc.gpsimd.tensor_tensor(zlow[:, :, :], zlow[:, :, :], zlneg[:, :, :], ALU.add)
                for t in range(CT):
                    for px in (slice(0, CH // 2), slice(CH // 2, CH)):
                        ins = nc.gpsimd.tensor_tensor(z[:, t, px], z[:, t, px], zneg[:, t, px], ALU.add)
                ins.then_inc(prelu_ready, 1)
                pool.wait_ge(prelu_ready, g + 1)
                for t in range(CT):
                    zr = z[:, t, :].rearrange("p (h two w s) -> p two h w s", h=HR, two=2, s=2)
                    for r in range(2):
                        ins = nc.gpsimd.tensor_tensor(zr[:, r], zr[:, r], spread(zlow, t), ALU.add)
                ins.then_inc(out_ready, 1)

            def turn(g, parity, c):
                split_frequencies(g)
                low_x(g)
                low_conv_in(g)
                add_up(g)

            turns(pool, turn, lambda image, parity: reduce_bound(image + 1))
            split_frequencies(ALL)
            low_conv_in(ALL)
            add_up(ALL)


def kernel(**inputs):
    import numpy as np
    import concourse.bacc as bacc
    from concourse.bass_utils import run_bass_kernel_spmd

    a = {k: np.asarray(v) for k, v in inputs.items()}
    both = [[a[f"L1_conv_{kind}_{p}"][:C] for kind in ("mag", "phase")] for p in ("b", "gamma", "beta", "mean", "var")]
    laid = {
        "x": a["x"].reshape(B, C, HW),
        "wqk": np.concatenate([a["L0_conv_Wq"], a["L0_conv_Wk"]]).T,
        "wv": a["L0_conv_Wv"],
        "wo": a["L0_conv_Wo"].T,
        "phase_w": a["L1_conv_phase_w"][:C].T,
        "mag_w": a["L1_conv_mag_w"].T,
        "params": np.stack([np.stack(p) for p in both]).reshape(5, 2, CT, 128).transpose(3, 0, 1, 2),
        "gamma": a["L0_conv_gamma"],
        "alpha": a["L1_conv_alpha"],
    }
    nc = bacc.Bacc("TRN2", target_bir_lowering=False, num_devices=1)
    arrays, args = {}, []
    for name, v in laid.items():
        v = np.ascontiguousarray(v)
        arrays[f"in_{name}"] = v
        args.append(nc.dram_tensor(f"in_{name}", v.shape, mybir.dt.from_np(v.dtype), kind="ExternalInput").ap())
    args.append(nc.dram_tensor("out_y", (B, C, HW), mybir.dt.float32, kind="ExternalOutput").ap())
    args.append(nc.dram_tensor("q_scratch", (NCH, DQK, CH), mybir.dt.float32, kind="Internal").ap())
    attention_conv(nc, *args)
    r = run_bass_kernel_spmd(nc, [arrays], core_ids=[0])
    return r.results[0]["out_y"].reshape(B, C, 64, 64)
```

```python
import concourse.bass as bass
from concourse import mybir
from contextlib import ExitStack

B, C, HW = 4, 256, 64 * 64
DQK = 32
CT = C // 128
CH = 512
NCH = HW // CH
MT = HW // 128
SUB = CH // 128
ALL = B * NCH
ROWS, WID = CH // 64, 64
LOWN = CH // 4
SCALE = DQK ** -0.5
EPS = 1e-5
SHIFT = 9.0
EVEN_FIRST = NCH // 2 + 1
UW = C + 1
LEAD = 2

ROUND_X, ROUND_CONV, SCAN, NEGATIVE = 9, 14, 12, 26
DOUBLE = (8, 10, 14, 16, 18, 22, 24, 26)
MAXIMA = [(j, m) for j in range(SUB) for m in range(NCH)]


class Plan:

    def __init__(self, steps, before=None):
        self.numbered, self.number = {}, {}
        for t, tasks in sorted(steps.items()):
            self.numbered[t] = [(len(self.number) + i, task) for i, task in enumerate(tasks)]
            self.number.update({task: n for n, task in self.numbered[t]})
        self.uses = len(self.number) // 2
        assert len(self.number) % 2 == 0
        kind, turns = before or (None, 0)
        self.first = kind.first + turns if kind else 0
        self.start = kind.start + kind.uses * turns if kind else 0


def steps_with_maxima(steps, first=4, doubled=DOUBLE):
    left = list(MAXIMA)
    t = first
    while left:
        for _ in range(2 if t in doubled else 1):
            steps.setdefault(t, []).append(("max",) + left.pop(0))
        t += 1
    steps[t + 1] = [("negmax",)]
    return steps


FULL = Plan(steps_with_maxima({0: [("kq",), ("u", 0)], 2: [("u", 1)], 5: [("y", 0)], 6: [("y", 1)], 19: [("low", 0)],
                               20: [("low", 1)], 21: [("high", 0)], 23: [("high", 1)]}))
LAST = Plan(steps_with_maxima({4: [("y", 0)], 5: [("y", 1)], 19: [("low", 0, 1)], 21: [("high", 0)], 23: [("high", 1)]},
                              first=3, doubled=(6, 8, 10, 12, 14, 16, 18, 24, 25)),
            before=(FULL, ALL - NCH))
FINAL = Plan({4: [("y", 0)], 5: [("y", 1)], 19: [("low", 0)], 20: [("low", 1)], 21: [("high", 0)], 23: [("high", 1)]},
             before=(LAST, NCH - 1))
TAIL = Plan({0: [("y", 0), ("y", 1), ("low", 0), ("low", 1), ("high", 0), ("high", 1)]}, before=(FINAL, 1))
MAXIMA_BY_KEYS = [(j, m) for m in range(NCH) for j in range(SUB)]
FIRST = [("wu", 0), ("wu", 1)] + [("max",) + jm for jm in MAXIMA_BY_KEYS] + [("negmax",)]


def attention_conv(nc, x, wqk, wv, wo, phase_w, mag_w, params, gamma, alpha, out, q_dram):
    f32, f32r, f16 = mybir.dt.float32, mybir.dt.float32r, mybir.dt.float16
    ALU, ACT, AX = mybir.AluOpType, mybir.ActivationFunctionType, mybir.AxisListType
    ds = bass.ds
    x_v = x.rearrange("b (t p) (k n) -> b k p t n", p=128, n=CH)
    out_v = out.rearrange("b (t p) (k n) -> b k p t n", p=128, n=CH)

    ctx = ExitStack()
    with ctx:
        def sb(name, shape, dt=f32):
            return ctx.enter_context(nc.sbuf_tensor(name, shape, dt))

        def sem(name):
            return ctx.enter_context(nc.semaphore(name))

        kst = sb("kst", [128, 2 * HW], f32r)
        uh_flat = [sb(f"uh{i}", [128, MT * UW], f16) for i in range(2)]
        uh = [buf[:, :].rearrange("p (m n) -> p m n", n=UW) for buf in uh_flat]
        ul = [sb(f"ul{i}", [128, MT, C], f16) for i in range(2)]
        wkq = [sb(f"wkq{i}", [128, CT, 4 * DQK], f32r) for i in range(2)]
        wu = [sb(f"wu{i}", [128, CT, C], f32r) for i in range(2)]
        wp = [sb(f"wp{i}", [128, 2 * CT, C], f32r) for i in range(2)]
        wm = [sb(f"wm{i}", [128, CT, C], f32r) for i in range(2)]
        ident = sb("ident", [128, 128])
        par = sb("par", [128, 5, 2, CT])
        var = sb("var", [128, 2, CT])
        half = sb("half", [128, 2, CT])
        spare = sb("spare", [128, 4])
        quarter = sb("quarter", [128, 1])
        rstd = sb("rstd", [128, 2, CT])
        bnA = sb("bnA", [128, 2, CT])
        bnB = sb("bnB", [128, 2, CT])
        al1 = sb("al1", [128, 1])
        gam = sb("gam", [128, 1])
        losel = sb("losel", [128, 1])
        amax = sb("amax", [128, 2, NCH])
        bnd = sb("bnd", [128, 1 + CT])
        bndall = sb("bndall", [128, 1 + CT])
        bndspare = sb("bndspare", [128, 1])
        prod = sb("prod", [128, 1])
        uscale = [sb(f"uscale{i}", [128, 1]) for i in range(2)]
        ogain = sb("ogain", [128, B])
        xb, xr, xs = sb("xb", [128, CT, CH]), sb("xr", [128, CT, CH]), sb("xs", [128, CT, CH])
        xbh, xbl = sb("xbh", [128, CT, CH], f32r), sb("xbl", [128, CT, CH], f32r)
        qsave = sb("qsave", [128, CH])
        qraw = sb("qraw", [96, CH])
        qst = sb("qst", [96, CH], f32r)
        qcur = sb("qcur", [128, CH], f32r)
        pmax = sb("pmax", [128, SUB, NCH])
        nmax = sb("nmax", [128, SUB])
        nhi = sb("nhi", [128, CH], f32r)
        p32 = sb("p32", [128, 2, CH])
        ph, pl = sb("ph", [128, 4, CH], f16), sb("pl", [128, 4, CH], f16)
        oraw = sb("oraw", [128, SUB, UW])
        rs = sb("rs", [128, SUB])
        on = sb("on", [128, SUB, C])
        y = sb("y", [128, CT, ROWS, WID])
        pair = sb("pair", [128, CT, ROWS, WID // 2])
        low4 = sb("low4", [128, CT, ROWS // 2, WID // 2])
        low = sb("low", [128, CT, LOWN])
        high = sb("high", [128, CT, ROWS, WID])
        hh, hl = [sb(n, [128, CT, ROWS + 1, WID], f32r) for n in ("hh", "hl")]
        lh, ll = [sb(n, [128, CT, LOWN], f32r) for n in ("lh", "ll")]
        zlow, zlneg = sb("zlow", [128, CT, LOWN]), sb("zlneg", [128, CT, LOWN])
        z, zneg = sb("z", [128, CT, CH]), sb("zneg", [128, CT, CH])
        wraw_p = high[:, :, :, :].rearrange("p t r w -> p (t r w)").rearrange("p (t n) -> p t n", n=C)
        wraw_m = p32[:, 0, :].rearrange("p (t n) -> p t n", n=C)
        wraw_v = p32[:, 1, :].rearrange("p (t n) -> p t n", n=C)
        wraw_o = on[:, 0:CT, :]
        wraw_qk = on[:, CT:2 * CT, 0:2 * DQK]
        x0 = [buf.bitcast(f32)[:, 0:HW].rearrange("p (i t n) -> p i t n", t=CT, n=CH)
              for buf in (ul[1][:, :, :].rearrange("p m n -> p (m n)"), uh_flat[1][:, :])]
        odd_hi, odd_lo = [buf[:, :, 1:ROWS + 1, :].rearrange("p t r w -> p t (r w)") for buf in (hh, hl)]

        O = [ctx.enter_context(nc.psum_tensor(f"O{i}", [128, 512], f32)) for i in range(SUB)]
        S = [ctx.enter_context(nc.psum_tensor(f"S{i}", [128, 512], f32)) for i in range(2)]
        M = [ctx.enter_context(nc.psum_tensor(f"M{i}", [128, 512], f32)) for i in range(2)]
        PK = [[O[0], O[1], O[2]], [O[3], S[0], S[1]]]

        w_loaded, conv_w_loaded, par_loaded = sem("w_loaded"), sem("conv_w_loaded"), sem("par_loaded")
        x0_loaded = [sem(f"x0_loaded{c}") for c in range(NCH)]
        scan_loaded, scanned = [sem("scan_even_loaded"), sem("scan_odd_loaded")], sem("scanned")
        xb_loaded, xr_loaded, xs_loaded = sem("xb_loaded"), sem("xr_loaded"), sem("xs_loaded")
        x_hi, x_split = [sem("even_hi"), sem("odd_hi")], [sem("even_split"), sem("odd_split")]
        qsave_ready, qsave_free, qraw_loaded, qst_ready = sem("qsave_ready"), sem("qsave_free"), sem("qraw_loaded"), sem("qst_ready")
        consts, pool_step = sem("consts"), sem("pool_step")
        conv_w_split = sem("conv_w_split")
        w_hi, conv_w_hi, w_split, wu_hi = sem("w_hi"), sem("conv_w_hi"), sem("w_split"), sem("wu_hi")
        bound, reduced, sstep, scaled, dstep = sem("bound"), sem("reduced"), sem("sstep"), sem("scaled"), sem("dstep")
        var_ready, bn_ready = sem("var_ready"), sem("bn_ready")
        proj_filled, proj_hi, proj_free = sem("proj_filled"), sem("proj_hi"), sem("proj_free")
        m_filled = [sem("m0_filled"), sem("m1_filled")]
        m_free = [sem("m0_free"), sem("m1_free")]
        q_hi, k_hi, u_hi, xs_scanned = sem("q_hi"), sem("k_hi"), sem("u_hi"), sem("xs_scanned")
        scanned0 = sem("scanned0")
        nmax_ready, nhi_ready = sem("nmax_ready"), sem("nhi_ready")
        s_filled, probs_ready, lo_ready, pv_done = sem("s_filled"), sem("probs_ready"), sem("lo_ready"), sem("pv_done")
        o_done = sem("o_done")
        o02_out, o13_out, rs_step, on_ready = sem("o02_out"), sem("o13_out"), sem("rs_step"), sem("on_ready")
        pairs_ready, low_ready, high_ready = sem("pairs_ready"), sem("low_ready"), sem("high_ready")
        hh_ready, conv_in = sem("hh_ready"), sem("conv_in")
        zneg_ready = sem("zneg_ready")
        prelu_ready, out_ready, out_stored = sem("prelu_ready"), sem("out_ready"), sem("out_stored")
        low4_ready, rstd_ready, banks_set, pmax_reduced = sem("low4_ready"), sem("rstd_ready"), sem("banks_set"), sem("pmax_reduced")

        FB = (len(FIRST) + 1) // 2, len(FIRST) // 2

        def use(plan, g, n):
            return plan.uses * g + (FB[n % 2] + plan.start - plan.uses * plan.first + n // 2)

        def emptied(eng, plan, g, *tasks):
            for task in tasks:
                n = plan.number[task]
                eng.wait_ge(m_free[n % 2], use(plan, g, n) + 1)

        def kind_of(plan, kind):
            return [task for task in plan.number if task[0] == kind]

        def turns(eng, turn, before_image=None, before_last=None):
            with eng.Fori(0, B // 2 - 1) as pair_i:
                for parity in range(2):
                    if before_image:
                        before_image(pair_i * 2 + parity, parity)
                    with eng.Fori(0, NCH) as c:
                        turn(pair_i * (2 * NCH) + parity * NCH + c, parity, c, FULL, scans=True)
            if before_image:
                before_image(B - 2, 0)
            with eng.Fori(0, NCH) as c:
                turn((B - 2) * NCH + c, 0, c, FULL, scans=False)
            if before_last:
                before_last()
            with eng.Fori(0, NCH - 1) as c:
                turn((B - 1) * NCH + c, 1, c, LAST, scans=False)
            turn(ALL - 1, 1, NCH - 1, FINAL, scans=False)

        HR = ROWS // 2

        def rows(buf, t, r):
            return buf[:, t, :, :].rearrange("p (h two) (w s) -> p two h w s", two=2, s=2)[:, r]

        def spread(buf, t):
            return buf[:, t, :].rearrange("p (h w a) -> p h w a", h=HR, a=1).to_broadcast([128, HR, WID // 2, 2])

        def split_frequencies(eng, ops, plan, g):
            emptied(eng, plan, g, ("y", 1))
            for t in range(CT):
                yp = y[:, t, :, :].rearrange("p r (w s) -> p s r w", s=2)
                ins = ops.tensor_tensor(pair[:, t, :, :], yp[:, 0], yp[:, 1], ALU.add)
            ins.then_inc(pairs_ready, 1)
            eng.wait_ge(pairs_ready, g + 1)
            pp = pair[:, :, :, :].rearrange("p t (h s) w -> p s (t h) w", s=2)
            ops.tensor_tensor(low4[:, :, :, :].rearrange("p t h w -> p (t h) w"), pp[:, 0], pp[:, 1],
                                    ALU.add).then_inc(low4_ready, 1)
            eng.wait_ge(low4_ready, g + 1)
            ops.tensor_tensor(low[:, :, :].rearrange("p t n -> p (t n)"),
                                    low4[:, :, :, :].rearrange("p t h w -> p (t h w)"),
                                    quarter[:, 0:1].to_broadcast([128, CT * LOWN]), ALU.mult).then_inc(low_ready, 1)
            eng.wait_ge(low_ready, g + 1)
            for t in range(CT):
                for r in range(2):
                    ins = ops.tensor_tensor(rows(high, t, r), rows(y, t, r), spread(low, t), ALU.subtract)
            ins.then_inc(high_ready, 1)

        def low_conv_in(eng, ops, g):
            eng.wait_ge(hh_ready, g + 1)
            for t in range(CT):
                for r in (0, HR):
                    ops.tensor_tensor(hl[:, t, 1 + r:1 + r + HR, :], high[:, t, r:r + HR, :],
                                            hh[:, t, 1 + r:1 + r + HR, :].bitcast(f32), ALU.subtract)
            ops.tensor_tensor(hl[:, :, 0, :], high[:, :, ROWS - 1, :], hh[:, :, 0, :].bitcast(f32), ALU.subtract)
            ops.tensor_tensor(ll[:, :, :], low[:, :, :], lh[:, :, :].bitcast(f32), ALU.subtract).then_inc(conv_in, 1)

        block = ctx.enter_context(nc.Block())

        @block.sync
        def _(sp):
            sp.dma_start(wraw_v, wv.rearrange("(t p) n -> p t n", p=128)).then_inc(w_loaded, 16)
            sp.dma_start(wraw_o, wo.rearrange("(t p) n -> p t n", p=128)).then_inc(w_loaded, 16)
            sp.dma_start(wraw_qk, wqk.rearrange("(t p) n -> p t n", p=128)).then_inc(w_loaded, 16)
            for c in range(2):
                sp.dma_start(x0[c % 2][:, c // 2], x_v[0, c]).then_inc(x0_loaded[c], 16)
            sp.dma_start(par[:, :, :, :], params).then_inc(par_loaded, 16)
            sp.dma_start(gam[:, :], gamma.partition_broadcast(128)).then_inc(par_loaded, 16)
            sp.dma_start(al1[:, :], alpha.partition_broadcast(128)).then_inc(par_loaded, 16)
            sp.dma_start(wraw_p, phase_w.rearrange("(t p) n -> p t n", p=128)).then_inc(conv_w_loaded, 16)
            sp.dma_start(wraw_m, mag_w.rearrange("(t p) n -> p t n", p=128)).then_inc(conv_w_loaded, 16)
            for c in range(2, NCH):
                sp.dma_start(x0[c % 2][:, c // 2], x_v[0, c]).then_inc(x0_loaded[c], 16)

            def fetch_q(slot):
                for s in range(3):
                    src = q_dram[slot] if isinstance(slot, int) else q_dram[slot].rearrange("k q n -> (k q) n")
                    sp.dma_start(qraw[s * DQK:(s + 1) * DQK, :], src).then_inc(qraw_loaded, 16)

            sp.dma_start(xr[:, :, :], x_v[1, 0]).then_inc(scan_loaded[0], 16)
            for c in range(NCH):
                sp.wait_ge(qsave_ready, c + 1)
                sp.dma_start(q_dram[c], qsave[96:128, :]).then_inc(qsave_free, 16)
                if c == 0:
                    sp.wait_ge(qsave_free, 16 * 2)
                    fetch_q(0)
                    sp.dma_start(xs[:, :, :], x_v[1, 1]).then_inc(scan_loaded[1], 16)
                    sp.dma_start(xb[:, :, :], x_v[1, 0]).then_inc(xb_loaded, 16)
                if c + 2 < NCH:
                    sp.wait_ge(scanned, c + 1)
                    sp.dma_start((xr, xs)[c % 2][:, :, :], x_v[1, c + 2]).then_inc(scan_loaded[c % 2], 16)
            sp.wait_ge(qsave_free, 16 * (NCH + 1))
            sp.wait_ge(qst_ready, 1)
            fetch_q(1)
            sp.wait_ge(scanned, NCH)
            sp.dma_start(xr[:, :, :], x_v[B - 1, NCH - 1]).then_inc(xr_loaded, 16)
            sp.dma_start(xs[:, :, :], x_v[2, 0]).then_inc(xs_loaded, 16)

            def turn(g, parity, c, plan, scans):
                if plan is FULL:
                    sp.wait_ge(qsave_ready, NCH + g + 1)
                    sp.dma_start(q_dram[ds(c, 1)].rearrange("k q n -> (k q) n"), qsave[96:128, :]).then_inc(qsave_free, 16)
                if plan is not FINAL:
                    sp.wait_ge(qst_ready, g + 2)
                    if plan is FULL:
                        sp.wait_ge(qsave_free, 16 * (NCH + g + 2))
                    fetch_q(ds((c + 2) % NCH, 1))
                if plan is FULL:
                    sp.wait_ge(x_split[0], EVEN_FIRST + g)
                    gk = (g + 1 + NCH) % ALL
                    sp.dma_start(xb[:, :, :], x_v[ds(gk // NCH, 1), ds(gk % NCH, 1)]).then_inc(xb_loaded, 16)
                emptied(sp, plan, g, ("y", 1))
                sp.dma_start(xr[:, :, :], x_v[ds(g // NCH, 1), ds(g % NCH, 1)]).then_inc(xr_loaded, 16)
                if scans:
                    sp.wait_ge(xs_scanned, g + 2)
                    gs = (g + 1 + 2 * NCH) % ALL
                    sp.dma_start(xs[:, :, :], x_v[ds(gs // NCH, 1), ds(gs % NCH, 1)]).then_inc(xs_loaded, 16)
                sp.wait_ge(out_ready, g + 2)
                gp = (g + (ALL - 1)) % ALL
                sp.dma_start(out_v[ds(gp // NCH, 1), ds(gp % NCH, 1)], z[:, :, :]).then_inc(out_stored, 16)

            turns(sp, turn)
            for o in range(CT):
                sp.wait_ge(out_ready, ALL + 2 + o)
                sp.dma_start(out_v[B - 1, NCH - 1][:, o], z[:, o, :]).then_inc(out_stored, 16)
            sp.wait_ge(out_stored, 16 * (ALL + 1 + CT))
            sp.wait_ge(xb_loaded, 16 * (1 + ALL - NCH))
            sp.wait_ge(xs_loaded, 16 * (1 + ALL - 2 * NCH))
            sp.wait_ge(xr_loaded, 16 * (1 + ALL))
            sp.wait_ge(qraw_loaded, 16 * 3 * (1 + ALL))
            sp.wait_ge(qsave_free, 16 * (1 + ALL))

        @block.tensor
        def _(pe):
            def wide(bank, stat, mov, last=None):
                products = [(a, b) for pa, pb in ((0, 0), (0, 1), (1, 0)) for a, b in zip(stat[pa], mov[pb])]
                for i, (a, b) in enumerate(products):
                    ins = nc.tensor.matmul(bank, a, b, start=(i == 0), stop=(i == len(products) - 1))
                return ins

            def project_kq(bank, xs):
                return wide(bank[:, :], [[wkq[v][:, t, :] for t in range(CT)] for v in range(2)],
                            [[xs[v][:, t, :] for t in range(CT)] for v in range(2)])

            def project_u(bank, xs, half_i):
                for m in range(2):
                    px = slice((2 * half_i + m) * 128, (2 * half_i + m + 1) * 128)
                    ins = wide(bank[:, m * C:(m + 1) * C], [[xs[v][:, t, px] for t in range(CT)] for v in range(2)],
                               [[wu[v][:, t, :] for t in range(CT)] for v in range(2)])
                return ins

            def transposed(bank, h):
                for j in range(SUB):
                    ins = nc.tensor.transpose(bank[:, j * 128:(j + 1) * 128], on[:, j, h * 128:(h + 1) * 128], ident[:, :])
                return ins

            def low_conv(bank, *tiles):
                for i, o in enumerate(tiles):
                    ins = wide(bank[:, i * LOWN:(i + 1) * LOWN],
                               [[wm[v][:, t, o * 128:(o + 1) * 128] for t in range(CT)] for v in range(2)],
                               [[(lh, ll)[v][:, t, :] for t in range(CT)] for v in range(2)])
                return ins

            def high_conv(bank, oh):
                return wide(bank[:, :], [[wp[v][:, s * CT + t, oh * 128:(oh + 1) * 128] for s in range(2) for t in range(CT)]
                                         for v in range(2)],
                            [[(hh, hl)[v][:, t, 1 - s:1 - s + ROWS, :].rearrange("p r w -> p (r w)")
                              for s in range(2) for t in range(CT)] for v in range(2)])

            def max_scores(bank, j, keys_at):
                return nc.tensor.matmul(bank[:, :], qst[:, j * 128:(j + 1) * 128], kst[0:96, keys_at],
                                        start=True, stop=True)

            def negmax_rows(bank):
                for j in range(SUB):
                    ins = nc.tensor.transpose(bank[:, j * 128:(j + 1) * 128],
                                              nmax[:, j:j + 1].to_broadcast([128, 128]), ident[:, :])
                return ins

            pe.wait_ge(w_loaded, 3 * 16)
            pe.wait_ge(consts, 1)
            for n in range(2):
                for t in range(CT):
                    ins = nc.tensor.matmul(M[n][:, 0:C], wraw_v[:, t, n * 128:(n + 1) * 128],
                                           wraw_o[:, t, :], start=(t == 0), stop=(t == CT - 1))
                ins.then_inc(m_filled[n], 1)
            nc.tensor.transpose(O[0][:, 0:128], ident[:, :], ident[:, :]).then_inc(pv_done, 1)
            pe.wait_ge(w_split, 4)
            for n in range(CT):
                pe.wait_ge(m_free[n], 1)

            def first_max(m, j):
                n = 2 + j
                pe.wait_ge(m_free[n % 2], SUB // 2 * m + n // 2)
                max_scores(M[n % 2], j, ds(m * CH, CH)).then_inc(m_filled[n % 2], 1)

            def first_projections(i, s, xs, with_maxima):
                m = 2 * i + s - 2
                pe.wait_ge(x_split[s], i + 1)
                pe.wait_ge(proj_free, 6 * i + 3 * s + 1)
                project_kq(PK[s][0], xs).then_inc(proj_filled, 1)
                if with_maxima:
                    pe.wait_ge(qst_ready, 1)
                    first_max(m, 0)
                    first_max(m, 1)
                for hf in range(2):
                    project_u(PK[s][1 + hf], xs, hf).then_inc(proj_filled, 1)
                if with_maxima:
                    first_max(m, 2)
                    first_max(m, 3)

            FIRST_X = ((0, (xbh, xbl)), (1, (odd_hi, odd_lo)))
            for s, xs in FIRST_X:
                first_projections(0, s, xs, False)
            with pe.Fori(1, NCH // 2) as i:
                for s, xs in FIRST_X:
                    first_projections(i, s, xs, True)
            pe.wait_ge(proj_free, 4 + 3 * NCH)
            for m in (NCH - 2, NCH - 1):
                for j in range(SUB):
                    first_max(m, j)
            n = len(FIRST) - 1
            pe.wait_ge(m_free[n % 2], n // 2)
            pe.wait_ge(nmax_ready, 1)
            negmax_rows(M[n % 2]).then_inc(m_filled[n % 2], 1)

            pe.wait_ge(conv_w_split, CT)
            pe.wait_ge(m_free[0], FB[0])

            def scores(g, parity, t):
                if t >= LEAD:
                    pe.wait_ge(probs_ready, MT * g + t - 1)
                at = parity * HW + t * 128
                nc.tensor.matmul(S[t % 2][:, :], kst[:, at:at + 128], qcur[:, :],
                                 start=True, stop=True).then_inc(s_filled, 1)

            def tasks(g, plan, keys_next, t):
                for n, task in plan.numbered.get(t, []):
                    kind = task[0]
                    bank = M[n % 2]
                    pe.wait_ge(m_free[n % 2], use(plan, g, n))
                    if kind in ("kq", "u"):
                        pe.wait_ge(x_split[0], EVEN_FIRST + g)
                        ins = project_kq(bank, (xbh, xbl)) if kind == "kq" else project_u(bank, (xbh, xbl), task[1])
                    elif kind == "y":
                        pe.wait_ge(on_ready, g + 2)
                        ins = transposed(bank, task[1])
                    elif kind == "low":
                        pe.wait_ge(conv_in, g + 1)
                        ins = low_conv(bank, *task[1:])
                    elif kind == "high":
                        ins = high_conv(bank, task[1])
                    elif kind == "max":
                        _, j, m = task
                        if (j, m) == MAXIMA[0]:
                            pe.wait_ge(qst_ready, g + 2)
                            if plan is FULL:
                                emptied(pe, plan, g, ("kq",))
                        ins = max_scores(bank, j, ds(keys_next + m * CH, CH))
                    else:
                        pe.wait_ge(nmax_ready, g + 2)
                        ins = negmax_rows(bank)
                    ins.then_inc(m_filled[n % 2], 1)

            def weigh(g, parity, t):
                pe.wait_ge(lo_ready, MT * g + t + 1)
                for j in range(SUB):
                    if t == 0:
                        pe.wait_ge((o02_out, o13_out)[j % 2], 2 * g + j // 2 + 1)
                    q = slice(j * 128, (j + 1) * 128)
                    nc.tensor.matmul(O[j][:, 0:UW], ph[:, t % 4, q], uh[parity][:, t, :], start=(t == 0), stop=False)
                    nc.tensor.matmul(O[j][:, 0:C], ph[:, t % 4, q], ul[parity][:, t, :], start=False, stop=False)
                    ins = nc.tensor.matmul(O[j][:, 0:UW], pl[:, t % 4, q], uh[parity][:, t, :],
                                           start=False, stop=(t == MT - 1))
                    if t == MT - 1 and j < SUB - 1:
                        ins.then_inc(o_done, 1)
                ins.then_inc(pv_done, 1)

            def first_scores(g, parity, plan):
                pe.wait_ge(m_free[1], use(plan, g, 1))
                for t in range(LEAD):
                    scores(g, parity, t)

            def turn(g, parity, c, plan, scans):
                keys_next = pe.snap(((c + (parity * NCH + 1)) // NCH) % 2 * HW) if plan is not FINAL else None
                if plan is FULL:
                    first_scores(g, parity, plan)
                for t in range(MT):
                    if t == 0:
                        tasks(g, plan, keys_next, t)
                    if t + LEAD < MT:
                        scores(g, parity, t + LEAD)
                    if t > 0:
                        tasks(g, plan, keys_next, t)
                    if t == MT - 1 and plan is LAST:
                        pe.wait_ge(m_free[1], use(plan, g + 1, 1))
                        pe.wait_ge(probs_ready, MT * g + MT - 1)
                        scores(g + 1, parity, 0)
                        pe.wait_ge(lo_ready, MT * g + MT)
                        scores(g + 1, parity, 1)
                    weigh(g, parity, t)

            turns(pe, turn, before_last=lambda: first_scores((B - 1) * NCH, 1, LAST))
            for n, task in TAIL.numbered[0]:
                pe.wait_ge(m_free[n % 2], use(TAIL, ALL, n))
                if task[0] == "y":
                    pe.wait_ge(on_ready, ALL + 2)
                    ins = transposed(M[n % 2], task[1])
                elif task[0] == "low":
                    pe.wait_ge(conv_in, ALL + 1)
                    ins = low_conv(M[n % 2], *task[1:])
                else:
                    ins = high_conv(M[n % 2], task[1])
                ins.then_inc(m_filled[n % 2], 1)

        @block.scalar
        def _(act):
            act.wait_ge(w_loaded, 3 * 16)
            for s in range(4):
                src = slice(DQK, 2 * DQK) if s < 3 else slice(0, DQK)
                nc.scalar.activation(wkq[0][:, :, s * DQK:(s + 1) * DQK], wraw_qk[:, :, src], ACT.Copy).then_inc(w_hi, 1)
            for n in range(CT):
                act.wait_ge(m_filled[n], 1)
                nc.scalar.activation(wu[0][:, n, :], M[n][:, 0:C], ACT.Copy).then_inc(wu_hi, 1)
            for s, hi in ((0, xbh[:, :, :]), (1, odd_hi)):
                act.wait_ge(x0_loaded[s], 16)
                nc.scalar.activation(hi, x0[s][:, 0], ACT.Copy).then_inc(x_hi[s], 1)
            act.wait_ge(conv_w_loaded, 2 * 16)
            nc.scalar.activation(wp[0][:, :, :], wraw_p, ACT.Copy)
            nc.scalar.activation(wm[0][:, :, :], wraw_m, ACT.Copy).then_inc(conv_w_hi, 1)

            def take_projections(i, s, first=False):
                filled = 6 * i + 3 * s
                act.wait_ge(proj_filled, filled + 1)
                nc.scalar.activation(kst[0:96, ds((2 * i + s) * CH, CH)], PK[s][0][0:96, :], ACT.Copy).then_inc(proj_hi, 1)
                act.wait_ge(qsave_free, 16 * (2 * i + s + 1))
                nc.scalar.activation(qsave[96:128, :], PK[s][0][96:128, :], ACT.Copy).then_inc(qsave_ready, 1)
                if first:
                    act.wait_ge(scaled, 1)
                for hf in range(2):
                    act.wait_ge(proj_filled, filled + 2 + hf)
                    nc.scalar.activation(uh[0][:, ds((2 * i + s) * SUB + 2 * hf, 2), 0:C],
                                         PK[s][1 + hf][:, :].rearrange("p (m n) -> p m n", n=C),
                                         ACT.Copy, scale=uscale[0][:, 0:1]).then_inc(proj_hi, 1)

            FIRST_HI = ((0, xbh[:, :, :]), (1, odd_hi))
            for s, hi in FIRST_HI:
                take_projections(0, s, first=(s == 0))
                if s == 0:
                    for c in range(2, NCH):
                        act.wait_ge(x0_loaded[c], 16)
                nc.scalar.activation(hi, x0[s][:, 1], ACT.Copy).then_inc(x_hi[s], 1)
            act.wait_ge(qraw_loaded, 16 * 3)
            nc.scalar.activation(qst[:, :], qraw[:, :], ACT.Copy).then_inc(q_hi, 1)
            with act.Fori(1, NCH // 2 - 1) as i:
                for s, hi in FIRST_HI:
                    take_projections(i, s)
                    nc.scalar.activation(hi, x0[s][:, ds(i + 1, 1)].rearrange("p i t n -> p (i t) n"), ACT.Copy).then_inc(x_hi[s], 1)
            take_projections(NCH // 2 - 1, 0)
            act.wait_ge(xb_loaded, 16)
            nc.scalar.activation(xbh[:, :, :], xb[:, :, :], ACT.Copy).then_inc(x_hi[0], 1)
            take_projections(NCH // 2 - 1, 1)
            act.wait_ge(conv_w_split, CT)
            act.wait_ge(bn_ready, 1)
            act.wait_ge(banks_set, 1)

            def copy_out(g, j):
                if j < SUB - 1:
                    act.wait_ge(o_done, (SUB - 1) * g + j + 1)
                else:
                    act.wait_ge(pv_done, MT * g + 1)
                act.wait_ge(on_ready, g + 1)
                nc.scalar.activation(oraw[:, j, :], O[j][:, 0:UW], ACT.Copy).then_inc(o02_out, 1)

            def probabilities(g, t):
                act.wait_ge(s_filled, MT * g + t + 1)
                if t >= 4:
                    act.wait_ge(pv_done, MT * g + t - 2)
                nc.scalar.activation(ph[:, t % 4, :], S[t % 2][:, :], ACT.Exp, scale=SCALE)
                if t >= 2:
                    act.wait_ge(lo_ready, MT * g + t - 1)
                nc.scalar.activation(p32[:, t % 2, :], S[t % 2][:, :], ACT.Exp, scale=SCALE).then_inc(probs_ready, 1)

            def take(bank, task, g, parity, c):
                kind = task[0]
                if kind == "kq":
                    nc.scalar.activation(kst[0:96, ds(c * CH + (1 - parity) * HW, CH)], bank[0:96, :], ACT.Copy).then_inc(k_hi, 1)
                    act.wait_ge(qsave_free, 16 * (NCH + g + 1))
                    nc.scalar.activation(qsave[96:128, :], bank[96:128, :], ACT.Copy).then_inc(qsave_ready, 1)
                elif kind == "u":
                    nc.scalar.activation(uh[1 - parity][:, ds(c * SUB + 2 * task[1], 2), 0:C],
                                         bank[:, :].rearrange("p (m n) -> p m n", n=C),
                                         ACT.Copy, scale=uscale[1 - parity][:, 0:1]).then_inc(u_hi, 1)

            def norm_low(bank, g, tiles, free):
                act.wait_ge(out_ready, g + 1)
                for i, o in enumerate(tiles):
                    ins = nc.scalar.activation(zlow[:, o, :], bank[:, i * LOWN:(i + 1) * LOWN], ACT.Identity,
                                               scale=bnA[:, 0, o:o + 1], bias=bnB[:, 0, o:o + 1])
                ins.then_inc(free, 1)

            def norm_high(bank, g, o, free):
                act.wait_ge(out_stored, 16 * g + 16)
                nc.scalar.activation(z[:, o, :], bank[:, :], ACT.Identity, scale=bnA[:, 1, o:o + 1],
                                     bias=bnB[:, 1, o:o + 1]).then_inc(free, 1)

            def round_conv(g):
                act.wait_ge(high_ready, g + 2)
                nc.scalar.activation(hh[:, :, 1:ROWS + 1, :], high[:, :, :, :], ACT.Copy)
                nc.scalar.activation(hh[:, :, 0, :], high[:, :, ROWS - 1, :], ACT.Copy)
                nc.scalar.activation(lh[:, :, :], low[:, :, :], ACT.Copy).then_inc(hh_ready, 1)

            def turn(g, parity, c, plan, scans):
                if plan is FULL:
                    copy_out(g, 0)
                probabilities(g, 0)
                if plan is not FULL:
                    copy_out(g, 0)
                copy_out(g, 2)
                probabilities(g, 1)
                for t in range(MT):
                    if 0 < t < MT - LEAD:
                        probabilities(g, t + LEAD)
                    for n, task in plan.numbered.get(t, []):
                        bank = M[n % 2]
                        if task[0] in ("kq", "u", "low", "high"):
                            act.wait_ge(m_filled[n % 2], use(plan, g, n) + 1)
                        if task[0] == "low":
                            norm_low(bank, g, task[1:], m_free[n % 2])
                        elif task[0] == "high":
                            norm_high(bank, g, task[1], m_free[n % 2])
                        else:
                            take(bank, task, g, parity, c)
                    if t == 0:
                        probabilities(g, LEAD)
                    if t == 0 and plan is not FINAL:
                        act.wait_ge(m_free[1], use(plan, g, 1))
                        act.wait_ge(qraw_loaded, 16 * 3 * (g + 2))
                        nc.scalar.activation(qst[:, :], qraw[:, :], ACT.Copy).then_inc(q_hi, 1)
                    if t == ROUND_X and plan is FULL:
                        act.wait_ge(xb_loaded, (g + 2) * 16)
                        nc.scalar.activation(xbh[:, :, :], xb[:, :, :], ACT.Copy).then_inc(x_hi[0], 1)
                    if t == ROUND_CONV:
                        round_conv(g)

            def before_image(image, parity):
                act.wait_ge(scaled, image + 2)

            turns(act, turn, before_image)
            copy_out(ALL, 0)
            copy_out(ALL, 2)
            round_conv(ALL)
            for n, task in TAIL.numbered[0]:
                if task[0] != "y":
                    act.wait_ge(m_filled[n % 2], use(TAIL, ALL, n) + 1)
                    if task[0] == "low":
                        norm_low(M[n % 2], ALL, task[1:], m_free[n % 2])
                    else:
                        norm_high(M[n % 2], ALL, task[1], m_free[n % 2])

        @block.vector
        def _(dve):
            chain = [0]

            def done(ins):
                chain[0] += 1
                ins.then_inc(dstep, 1)
                dve.wait_ge(dstep, chain[0])

            nc.vector.memset(half[:, :, :], -0.5).then_inc(on_ready, 1)
            nc.vector.memset(quarter[:, :], 0.25).then_inc(out_stored, 16)
            nc.vector.memset(uh[0][:, :, C:C + 1], 1.0).then_inc(qsave_free, 16)
            nc.vector.memset(ogain[:, :], 1.0).then_inc(xs_scanned, 1)
            nc.vector.memset(spare[:, 2:3], 0.0).then_inc(proj_free, 4)
            nc.vector.memset(spare[:, 3:4], 0.0).then_inc(o_done, SUB - 1)
            dve.wait_ge(consts, 1)
            done(nc.vector.tensor_tensor(prod[:, :], ident[:, 96:97], ident[:, 97:98], ALU.add))
            nc.vector.tensor_scalar(kst[96:128, :], ident[96:128, 0:1].to_broadcast([32, 2 * HW]), 0.0,
                                    prod[96:128, 0:1], ALU.mult, ALU.add)
            done(nc.vector.tensor_scalar(losel[:, :], ident[:, 96:97], 1.0, None, ALU.subtract))
            dve.wait_ge(w_hi, 4)
            for s in range(4):
                src = slice(DQK, 2 * DQK) if s < 3 else slice(0, DQK)
                cols = slice(s * DQK, (s + 1) * DQK)
                nc.vector.tensor_tensor(wkq[1][:, :, cols], wraw_qk[:, :, src], wkq[0][:, :, cols].bitcast(f32),
                                        ALU.subtract).then_inc(w_split, 1)
            for n in range(CT):
                dve.wait_ge(wu_hi, n + 1)
                nc.vector.tensor_reduce(bnd[:, 1 + n:2 + n], M[n][:, 0:C], AX.X, ALU.max, apply_absolute_value=True)
                nc.vector.tensor_tensor(wu[1][:, n, :], M[n][:, 0:C], wu[0][:, n, :].bitcast(f32),
                                        ALU.subtract).then_inc(m_free[n], 1)

            def scan(at, xs, counted):
                nc.vector.tensor_reduce(at, xs.rearrange("p t n -> p (t n)"), AX.X, ALU.max,
                                        apply_absolute_value=True).then_inc(counted, 1)

            def find_scale(image, parity):
                nc.vector.tensor_reduce(bnd[:, 0:1], amax[:, parity, :], AX.X, ALU.max).then_inc(bound, 1)
                dve.wait_ge(reduced, image + 1)
                nc.vector.tensor_tensor(prod[:, :], bndall[:, 1:2], bndall[:, 2:3], ALU.max).then_inc(sstep, 1)
                dve.wait_ge(sstep, 3 * image + 1)
                nc.vector.tensor_tensor(prod[:, :], prod[:, :], bndall[:, 0:1], ALU.mult).then_inc(sstep, 1)
                dve.wait_ge(sstep, 3 * image + 2)
                nc.vector.tensor_scalar(prod[:, :], prod[:, :], C / 2.0 ** 15, 1e-30, ALU.mult, ALU.max).then_inc(sstep, 1)
                dve.wait_ge(sstep, 3 * image + 3)
                gain = ogain[:, ds(image, 1)]
                nc.vector.tensor_tensor(gain, prod[:, :], gam[:, :], ALU.mult)
                nc.vector.reciprocal(uscale[parity][:, :], prod[:, :]).then_inc(scaled, 1)

            for c in range(NCH):
                dve.wait_ge(x0_loaded[c], 16)
                scan(amax[:, 0, c:c + 1], x0[c % 2][:, c // 2], scanned0)
            dve.wait_ge(par_loaded, 3 * 16)
            dve.wait_ge(scanned0, NCH)
            find_scale(0, 0)

            done(nc.vector.tensor_scalar(var[:, :, :], par[:, 4, :, :], EPS, None, ALU.add))
            nc.vector.tensor_scalar(al1[:, :], al1[:, :], 1.0, None, ALU.subtract).then_inc(var_ready, 1)
            dve.wait_ge(rstd_ready, 1)
            done(nc.vector.tensor_tensor(bnA[:, :, :], par[:, 1, :, :], rstd[:, :, :], ALU.mult))
            done(nc.vector.tensor_tensor(bnB[:, :, :], par[:, 0, :, :], par[:, 3, :, :], ALU.subtract))
            done(nc.vector.tensor_tensor(bnB[:, :, :], bnB[:, :, :], bnA[:, :, :], ALU.mult))
            nc.vector.tensor_tensor(bnB[:, :, :], bnB[:, :, :], par[:, 2, :, :], ALU.add).then_inc(bn_ready, 1)

            def take_projection(i, s, step):
                dve.wait_ge(proj_hi, 6 * i + 3 * s + step + 1)
                if step == 0:
                    keys = kst[32:64, ds((2 * i + s) * CH, CH)]
                    nc.vector.tensor_tensor(keys, PK[s][0][32:64, :], keys.bitcast(f32), ALU.subtract).then_inc(proj_free, 1)
                else:
                    tiles = ds((2 * i + s) * SUB + 2 * (step - 1), 2)
                    nc.vector.scalar_tensor_tensor(ul[0][:, tiles, :], PK[s][step][:, :].rearrange("p (m n) -> p m n", n=C),
                                                   uscale[0][:, 0:1], uh[0][:, tiles, 0:C], ALU.mult, ALU.subtract)\
                        .then_inc(proj_free, 1)

            def low_q(count):
                dve.wait_ge(q_hi, count)
                nc.vector.tensor_tensor(qst[64:96, :], qraw[64:96, :], qst[64:96, :].bitcast(f32),
                                        ALU.subtract).then_inc(qst_ready, 1)

            def partial_max(bank, j, m, free):
                nc.vector.tensor_reduce(pmax[:, j, ds(m, 1)], bank[:, :], AX.X, ALU.max).then_inc(free, 1)

            def maxima(count):
                nc.vector.tensor_reduce(nmax[:, :], pmax[:, :, :], AX.X, ALU.max, negate=True).then_inc(pmax_reduced, 1)
                dve.wait_ge(pmax_reduced, count)
                nc.vector.tensor_scalar(nmax[:, :], nmax[:, :], SHIFT / SCALE, None, ALU.add).then_inc(nmax_ready, 1)

            def finish_q(bank, count, free):
                dve.wait_ge(nhi_ready, count)
                nc.vector.tensor_copy(qcur[0:96, :], qst[:, :].bitcast(f32))
                nc.vector.scalar_tensor_tensor(qcur[96:128, :], nhi[96:128, :].bitcast(f32), losel[96:128, 0:1],
                                               bank[96:128, :], ALU.mult, ALU.add).then_inc(free, 1)

            def scan_next(i, s):
                dve.wait_ge(scan_loaded[s], (i + 1) * 16)
                scan(amax[:, 1, ds(2 * i + s, 1)], (xr, xs)[s][:, :, :], scanned)

            def first_max(m, j):
                n = 2 + j
                dve.wait_ge(m_filled[n % 2], SUB // 2 * m + n // 2 + 1)
                partial_max(M[n % 2], j, m, m_free[n % 2])

            def first_chunk(i, s):
                for step in range(3):
                    take_projection(i, s, step)
                    for j in ((0, 1), (), (2, 3))[step]:
                        first_max(2 * i + s - 2, j)

            for s in range(2):
                for step in range(3):
                    take_projection(0, s, step)
                if s == 0:
                    scan_next(0, 0)
            low_q(1)
            scan_next(0, 1)
            with dve.Fori(1, NCH // 2) as i:
                for s in range(2):
                    first_chunk(i, s)
                    scan_next(i, s)
            dve.wait_ge(proj_free, 4 + 3 * NCH)
            nc.vector.memset(uh[1][:, :, C:C + 1], 1.0)
            for j in range(SUB):
                ins = nc.vector.memset(O[j][:, C:C + 1], 1.0)
            ins.then_inc(banks_set, 1)

            for m in (NCH - 2, NCH - 1):
                for j in range(SUB):
                    first_max(m, j)
            n = len(FIRST) - 1
            dve.wait_ge(m_free[(n - 1) % 2], (n - 1) // 2 + 1)
            maxima(1)
            dve.wait_ge(m_filled[n % 2], n // 2 + 1)
            nc.vector.tensor_copy(nhi[96:128, :], M[n % 2][96:128, :]).then_inc(nhi_ready, 1)
            finish_q(M[n % 2], 1, m_free[n % 2])
            dve.wait_ge(scanned, NCH)

            def copy_out(g, j):
                if j < SUB - 1:
                    dve.wait_ge(o_done, (SUB - 1) * g + j + 1)
                else:
                    dve.wait_ge(pv_done, MT * g + 1)
                dve.wait_ge(on_ready, g + 1)
                nc.vector.tensor_copy(oraw[:, j, :], O[j][:, 0:UW]).then_inc(o13_out, 1)

            def normalise(g):
                dve.wait_ge(o02_out, 2 * g + 2)
                dve.wait_ge(o13_out, 2 * g + 2)
                nc.vector.reciprocal(rs[:, :], oraw[:, :, C]).then_inc(rs_step, 1)
                dve.wait_ge(rs_step, 2 * g + 1)
                gain = ogain[:, B - 1:B] if isinstance(g, int) else ogain[:, ds((g + (ALL - 1)) % ALL // NCH, 1)]
                nc.vector.tensor_tensor(rs[:, :], rs[:, :], gain.to_broadcast([128, SUB]), ALU.mult).then_inc(rs_step, 1)
                dve.wait_ge(rs_step, 2 * g + 2)
                for j in range(SUB):
                    ins = nc.vector.tensor_scalar(on[:, j, :], oraw[:, j, 0:C], rs[:, j:j + 1], None, ALU.mult)
                ins.then_inc(on_ready, 1)

            def low_probabilities(g, t):
                dve.wait_ge(probs_ready, MT * g + t + 1)
                nc.vector.tensor_tensor(pl[:, t % 4, :], p32[:, t % 2, :], ph[:, t % 4, :], ALU.subtract).then_inc(lo_ready, 1)

            def add_residual(bank, g, h, free):
                if h == 0:
                    dve.wait_ge(xr_loaded, 16 * g + 16)
                    dve.wait_ge(high_ready, g + 1)
                nc.vector.tensor_tensor(y[:, h, :, :].rearrange("p r w -> p (r w)"), bank[:, :], xr[:, h, :],
                                        ALU.add).then_inc(free, 1)

            def negative_parts(plan, g):
                emptied(dve, plan, g, *kind_of(plan, "low"))
                nc.vector.tensor_scalar(zlneg[:, :, :], zlow[:, :, :], 0.0, al1[:, 0:1], ALU.min, ALU.mult)
                emptied(dve, plan, g, *kind_of(plan, "high"))
                nc.vector.tensor_scalar(zneg[:, :, :], z[:, :, :], 0.0, al1[:, 0:1], ALU.min, ALU.mult).then_inc(zneg_ready, 1)

            def take(n, task, g, parity, c, plan):
                kind, bank, free = task[0], M[n % 2], m_free[n % 2]
                if kind == "kq":
                    dve.wait_ge(k_hi, g + 1)
                    dve.wait_ge(qsave_ready, NCH + g + 1)
                    keys = kst[32:64, ds(c * CH + (1 - parity) * HW, CH)]
                    nc.vector.tensor_tensor(keys, bank[32:64, :], keys.bitcast(f32), ALU.subtract).then_inc(free, 1)
                elif kind == "u":
                    dve.wait_ge(u_hi, 2 * g + 1 + task[1])
                    tiles = ds(c * SUB + 2 * task[1], 2)
                    nc.vector.scalar_tensor_tensor(ul[1 - parity][:, tiles, :], bank[:, :].rearrange("p (m n) -> p m n", n=C),
                                                   uscale[1 - parity][:, 0:1], uh[1 - parity][:, tiles, 0:C], ALU.mult, ALU.subtract)\
                        .then_inc(free, 1)
                elif kind in ("y", "max", "negmax"):
                    dve.wait_ge(m_filled[n % 2], use(plan, g, n) + 1)
                    if kind == "y":
                        add_residual(bank, g, task[1], free)
                    elif kind == "max":
                        partial_max(bank, task[1], task[2], free)
                        if task[1:] == MAXIMA[-1]:
                            emptied(dve, plan, g, task)
                            maxima(g + 2)
                    else:
                        nc.vector.tensor_copy(nhi[96:128, :], bank[96:128, :]).then_inc(nhi_ready, 1)

            def finish_chunk(g):
                dve.wait_ge(s_filled, MT * g + MT)
                finish_q(M[1], g + 2, m_free[1])

            def turn(g, parity, c, plan, scans):
                if plan is not FULL:
                    low_probabilities(g, 0)
                copy_out(g, 1)
                copy_out(g, 3)
                if plan is FULL:
                    low_probabilities(g, 0)
                for t in range(MT):
                    if t == MT - 2 and plan is LAST:
                        finish_chunk(g)
                    if t + 1 < MT:
                        low_probabilities(g, t + 1)
                    if t == (0 if plan is FULL else 1):
                        normalise(g)
                    if t == 1 and plan is not FINAL:
                        low_q(g + 2)
                    if t == SCAN and scans:
                        dve.wait_ge(xs_loaded, (g + 1) * 16)
                        scan(amax[:, parity, ds(c, 1)], xs[:, :, :], xs_scanned)
                    for n, task in plan.numbered.get(t, []):
                        take(n, task, g, parity, c, plan)
                    if t == NEGATIVE:
                        negative_parts(plan, g)
                if plan is FULL:
                    finish_chunk(g)

            def before_image(image, parity):
                dve.wait_ge(xs_scanned, image * NCH + 1)
                find_scale(image + 1, 1 - parity)

            turns(dve, turn, before_image)
            copy_out(ALL, 1)
            copy_out(ALL, 3)
            normalise(ALL)
            for n, task in TAIL.numbered[0][:CT]:
                dve.wait_ge(m_filled[n % 2], use(TAIL, ALL, n) + 1)
                add_residual(M[n % 2], ALL, task[1], m_free[n % 2])
            split_frequencies(dve, nc.vector, TAIL, ALL)
            low_conv_in(dve, nc.vector, ALL)
            emptied(dve, TAIL, ALL, *kind_of(TAIL, "low"))
            nc.vector.tensor_scalar(zlneg[:, :, :], zlow[:, :, :], 0.0, al1[:, 0:1], ALU.min, ALU.mult).then_inc(zneg_ready, 1)
            dve.wait_ge(zneg_ready, ALL + 1)
            nc.vector.tensor_tensor(zlow[:, :, :], zlow[:, :, :], zlneg[:, :, :], ALU.add).then_inc(prelu_ready, 1)
            for o in range(CT):
                emptied(dve, TAIL, ALL, ("high", o))
                nc.vector.tensor_scalar(zneg[:, o, :], z[:, o, :], 0.0, al1[:, 0:1], ALU.min, ALU.mult).then_inc(zneg_ready, 1)
                dve.wait_ge(zneg_ready, ALL + 2 + o)
                nc.vector.tensor_tensor(z[:, o, :], z[:, o, :], zneg[:, o, :], ALU.add).then_inc(prelu_ready, 1)
                dve.wait_ge(prelu_ready, ALL + 2 + o)
                zr = z[:, o, :].rearrange("p (h two w s) -> p two h w s", h=HR, two=2, s=2)
                for r in range(2):
                    ins = nc.vector.tensor_tensor(zr[:, r], zr[:, r], spread(zlow, o), ALU.add)
                ins.then_inc(out_ready, 1)

        @block.gpsimd
        def _(pool):
            nc.gpsimd.memset(ident[:, :], 0.0).then_inc(pool_step, 1)
            pool.wait_ge(pool_step, 1)
            nc.gpsimd.affine_select(out=ident[:, :], in_=ident[:, :], compare_op=ALU.not_equal, fill=1.0, base=0,
                                    pattern=[[-1, 128]], channel_multiplier=1).then_inc(consts, 1)
            nc.gpsimd.memset(spare[:, 0:1], 0.0).then_inc(out_ready, 1)
            nc.gpsimd.memset(spare[:, 1:2], 0.0).then_inc(high_ready, 1)
            def low_x(s, lo, xs, hi, count):
                pool.wait_ge(x_hi[s], count)
                for t in range(CT):
                    for px in (slice(0, CH // 2), slice(CH // 2, CH)):
                        ins = nc.gpsimd.tensor_tensor(lo[:, t, px], xs[:, t, px], hi[:, t, px].bitcast(f32), ALU.subtract)
                ins.then_inc(x_split[s], 1)

            def low_x0(c):
                s = c % 2
                xs = x0[s][:, c // 2] if c < NCH else xb[:, :, :]
                low_x(s, (xbl[:, :, :], odd_lo)[s], xs, (xbh[:, :, :], odd_hi)[s], c // 2 + 1)

            def reduce_bound(image):
                pool.wait_ge(bound, image + 1)
                nc.gpsimd.tensor_tensor(bndspare[:, :], bnd[:, 0:1], bnd[:, 0:1], ALU.add)
                nc.gpsimd.partition_all_reduce(bndall[:, :], bnd[:, :], 128, bass.bass_isa.ReduceOp.max).then_inc(reduced, 1)

            low_x0(0)
            low_x0(1)
            reduce_bound(0)
            pool.wait_ge(var_ready, 1)
            nc.gpsimd.tensor_tensor(rstd[:, :, :], var[:, :, :], half[:, :, :], ALU.pow).then_inc(rstd_ready, 1)
            for c in range(2, NCH + 1):
                low_x0(c)
            pool.wait_ge(conv_w_hi, 1)
            for i in range(CT):
                for t in (2 * i, 2 * i + 1):
                    nc.gpsimd.tensor_tensor(wp[1][:, t, :], wraw_p[:, t, :], wp[0][:, t, :].bitcast(f32), ALU.subtract)
                nc.gpsimd.tensor_tensor(wm[1][:, i, :], wraw_m[:, i, :], wm[0][:, i, :].bitcast(f32),
                                        ALU.subtract).then_inc(conv_w_split, 1)

            def add_up(g):
                pool.wait_ge(zneg_ready, g + 1)
                nc.gpsimd.tensor_tensor(zlow[:, :, :], zlow[:, :, :], zlneg[:, :, :], ALU.add)
                for t in range(CT):
                    for px in (slice(0, CH // 2), slice(CH // 2, CH)):
                        ins = nc.gpsimd.tensor_tensor(z[:, t, px], z[:, t, px], zneg[:, t, px], ALU.add)
                ins.then_inc(prelu_ready, 1)
                pool.wait_ge(prelu_ready, g + 1)
                for t in range(CT):
                    zr = z[:, t, :].rearrange("p (h two w s) -> p two h w s", h=HR, two=2, s=2)
                    for r in range(2):
                        ins = nc.gpsimd.tensor_tensor(zr[:, r], zr[:, r], spread(zlow, t), ALU.add)
                ins.then_inc(out_ready, 1)

            def turn(g, parity, c, plan, scans):
                split_frequencies(pool, nc.gpsimd, plan, g)
                if plan is FULL:
                    low_x(0, xbl, xb, xbh, g + EVEN_FIRST + 1)
                low_conv_in(pool, nc.gpsimd, g)
                add_up(g)

            turns(pool, turn, lambda image, parity: reduce_bound(image + 1))


def kernel(**inputs):
    import numpy as np
    import concourse.bacc as bacc
    from concourse.bass_utils import run_bass_kernel_spmd

    a = {k: np.asarray(v) for k, v in inputs.items()}
    both = [[a[f"L1_conv_{kind}_{p}"][:C] for kind in ("mag", "phase")] for p in ("b", "gamma", "beta", "mean", "var")]
    laid = {
        "x": a["x"].reshape(B, C, HW),
        "wqk": np.concatenate([a["L0_conv_Wq"], a["L0_conv_Wk"]]).T,
        "wv": a["L0_conv_Wv"],
        "wo": a["L0_conv_Wo"].T,
        "phase_w": a["L1_conv_phase_w"][:C].T,
        "mag_w": a["L1_conv_mag_w"].T,
        "params": np.stack([np.stack(p) for p in both]).reshape(5, 2, CT, 128).transpose(3, 0, 1, 2),
        "gamma": a["L0_conv_gamma"],
        "alpha": a["L1_conv_alpha"],
    }
    nc = bacc.Bacc("TRN2", target_bir_lowering=False, num_devices=1)
    arrays, args = {}, []
    for name, v in laid.items():
        v = np.ascontiguousarray(v)
        arrays[f"in_{name}"] = v
        args.append(nc.dram_tensor(f"in_{name}", v.shape, mybir.dt.from_np(v.dtype), kind="ExternalInput").ap())
    args.append(nc.dram_tensor("out_y", (B, C, HW), mybir.dt.float32, kind="ExternalOutput").ap())
    args.append(nc.dram_tensor("q_scratch", (NCH, DQK, CH), mybir.dt.float32, kind="Internal").ap())
    attention_conv(nc, *args)
    r = run_bass_kernel_spmd(nc, [arrays], core_ids=[0])
    return r.results[0]["out_y"].reshape(B, C, 64, 64)
```
